# Optimizing a Trainium2 kernel written in Bass

```python
import numpy as np
import jax
import jax.numpy as jnp

def _softmax(x, axis=-1):
    return jax.nn.softmax(x, axis=axis)

def _gelu(x):
    return jax.nn.gelu(x, approximate=True)

def _silu(x):
    return jax.nn.silu(x)

def _sigmoid(x):
    return jax.nn.sigmoid(x)

def _layernorm(x, axis=-1, eps=1e-05):
    m = jnp.mean(x, axis=axis, keepdims=True)
    v = jnp.var(x, axis=axis, keepdims=True)
    return (x - m) / jnp.sqrt(v + eps)

def _scatter_add(tgt, idx, src, axis=0):
    return tgt.at[idx].add(src)

def _segment_sum(src, seg, n):
    return jax.ops.segment_sum(src, seg, n)
kernel_name = 'mk_flamingo_gated_d1_seqx_r4_0173ec'

def setup_inputs(seed: int=0):
    np.random.seed(seed)
    _w = jnp.asarray

    def _rec_inputs():
        import jax
        import jax.numpy as jnp
        _rk = jax.random.key(seed)
        x = 7.22e-05 + 1 * jax.random.normal(jax.random.fold_in(_rk, 1), (4, 512, 256), jnp.float32)
        _lenS = 512 - jax.random.randint(jax.random.fold_in(_rk, 7), (4,), 0, max(1, 512 // 4) + 1, jnp.int32)
        _lenS2 = 512 - jax.random.randint(jax.random.fold_in(_rk, 8), (4,), 0, max(1, 512 // 4) + 1, jnp.int32)
        _ctx_1024P = jax.random.normal(jax.random.fold_in(_rk, 11), (4, 16, 256), jnp.float32)
        _ctx_1024c = jax.random.dirichlet(jax.random.fold_in(_rk, 511), 0.3 * jnp.ones((16,), jnp.float32), (4, 512))
        _ctx_1024t = jnp.einsum('bsk,bkd->bsd', _ctx_1024c, _ctx_1024P)
        _ctx_1024t = _ctx_1024t * jax.lax.rsqrt(jnp.mean(jnp.square(_ctx_1024t)) + 1e-12) * 0.953939
        ctx_1024 = 4.13588e-05 + 0.999923 * (_ctx_1024t + 0.3 * jax.random.normal(jax.random.fold_in(_rk, 611), (4, 512, 256), jnp.float32))
        _g = jax.random.normal(jax.random.fold_in(_rk, 9001), (2, 1), jnp.float32)
        _g = jnp.sign(_g) * jnp.maximum(jnp.abs(_g), 1.0) + (_g == 0) * 1.0
        g_xattn = _g[0]
        g_ffn = _g[1]
        return (x, ctx_1024, g_xattn, g_ffn)
    x, ctx_1024, g_xattn, g_ffn = _rec_inputs()

    def _L0_xattn_setup():
        import jax, jax.numpy as jnp
        import numpy as np
        D_MODEL = 256
        NUM_HEADS = 16
        D_K = D_MODEL // NUM_HEADS

        def _split_heads(x):
            B, S, _ = x.shape
            return x.reshape(B, S, NUM_HEADS, D_K).transpose(0, 2, 1, 3)
        key = jax.random.key(seed)
        ks = jax.random.split(key, 11)
        B, S = (4, 512)
        s = 1.0 / np.sqrt(D_MODEL)
        return {'Q': jax.random.normal(ks[0], (B, S, D_MODEL), jnp.float32), 'K': jax.random.normal(ks[1], (B, S, D_MODEL), jnp.float32), 'V': jax.random.normal(ks[2], (B, S, D_MODEL), jnp.float32), 'Wq': jax.random.normal(ks[3], (D_MODEL, D_MODEL), jnp.float32) * s, 'bq': jax.random.normal(ks[4], (D_MODEL,), jnp.float32) * 0.01, 'Wk': jax.random.normal(ks[5], (D_MODEL, D_MODEL), jnp.float32) * s, 'bk': jax.random.normal(ks[6], (D_MODEL,), jnp.float32) * 0.01, 'Wv': jax.random.normal(ks[7], (D_MODEL, D_MODEL), jnp.float32) * s, 'bv': jax.random.normal(ks[8], (D_MODEL,), jnp.float32) * 0.01, 'Wo': jax.random.normal(ks[9], (D_MODEL, D_MODEL), jnp.float32) * s, 'bo': jax.random.normal(ks[10], (D_MODEL,), jnp.float32) * 0.01}
    _L0_xattn_all = _L0_xattn_setup()
    _L0_xattn_in = {k: v for k, v in _L0_xattn_all.items() if k in ('Wq', 'bq', 'Wk', 'bk', 'Wv', 'bv', 'Wo', 'bo')}
    del _L0_xattn_all

    def _L0_ffn_setup():
        import jax, jax.numpy as jnp
        import numpy as np
        E = 8
        TOPK = 2
        H = 256
        I = 256
        ISH = I * 2
        B, S = (2, 256)
        key = jax.random.key(seed)
        ks = jax.random.split(key, 7)
        s = 0.02
        return {'hidden_states': jax.random.normal(ks[0], (B, S, H), jnp.float32), 'w_router': jax.random.normal(ks[1], (H, E), jnp.float32) * s, 'fc1_w': jax.random.normal(ks[2], (E, H, 2 * I), jnp.float32) * s, 'fc2_w': jax.random.normal(ks[3], (E, I, H), jnp.float32) * s, 'gate_w': jax.random.normal(ks[4], (H, ISH), jnp.float32) * s, 'up_w': jax.random.normal(ks[5], (H, ISH), jnp.float32) * s, 'down_w': jax.random.normal(ks[6], (ISH, H), jnp.float32) * s}
    _L0_ffn_all = _L0_ffn_setup()
    _L0_ffn_in = {k: v for k, v in _L0_ffn_all.items() if k in ('w_router', 'fc1_w', 'fc2_w', 'gate_w', 'up_w', 'down_w')}
    del _L0_ffn_all
    return {'x': x, 'ctx_1024': ctx_1024, 'g_xattn': g_xattn, 'g_ffn': g_ffn, 'L0_xattn_Wq': _L0_xattn_in['Wq'], 'L0_xattn_bq': _L0_xattn_in['bq'], 'L0_xattn_Wk': _L0_xattn_in['Wk'], 'L0_xattn_bk': _L0_xattn_in['bk'], 'L0_xattn_Wv': _L0_xattn_in['Wv'], 'L0_xattn_bv': _L0_xattn_in['bv'], 'L0_xattn_Wo': _L0_xattn_in['Wo'], 'L0_xattn_bo': _L0_xattn_in['bo'], 'L0_ffn_w_router': _L0_ffn_in['w_router'], 'L0_ffn_fc1_w': _L0_ffn_in['fc1_w'], 'L0_ffn_fc2_w': _L0_ffn_in['fc2_w'], 'L0_ffn_gate_w': _L0_ffn_in['gate_w'], 'L0_ffn_up_w': _L0_ffn_in['up_w'], 'L0_ffn_down_w': _L0_ffn_in['down_w']}

def reference(x, ctx_1024, g_xattn, g_ffn, L0_xattn_Wq, L0_xattn_bq, L0_xattn_Wk, L0_xattn_bk, L0_xattn_Wv, L0_xattn_bv, L0_xattn_Wo, L0_xattn_bo, L0_ffn_w_router, L0_ffn_fc1_w, L0_ffn_fc2_w, L0_ffn_gate_w, L0_ffn_up_w, L0_ffn_down_w):
    import jax
    import jax.numpy as jnp

    def _L0_xattn_ref(Q, K, V, Wq, bq, Wk, bk, Wv, bv, Wo, bo):
        import jax, jax.numpy as jnp
        import numpy as np
        D_MODEL = 256
        NUM_HEADS = 16
        D_K = D_MODEL // NUM_HEADS

        def _split_heads(x):
            B, S, _ = x.shape
            return x.reshape(B, S, NUM_HEADS, D_K).transpose(0, 2, 1, 3)
        q = _split_heads(Q @ Wq.T + bq)
        k = _split_heads(K @ Wk.T + bk)
        v = _split_heads(V @ Wv.T + bv)
        scale = 1.0 / jnp.sqrt(jnp.asarray(D_K, jnp.float32))
        scores = jnp.einsum('bhqd,bhkd->bhqk', q, k) * scale
        attn = jax.nn.softmax(scores, axis=-1)
        ctx = jnp.einsum('bhqk,bhkd->bhqd', attn, v)
        B, H, S, Dk = ctx.shape
        ctx = ctx.transpose(0, 2, 1, 3).reshape(B, S, H * Dk)
        return ctx @ Wo.T + bo

    def _L0_ffn_ref(hidden_states, w_router, fc1_w, fc2_w, gate_w, up_w, down_w):
        import jax, jax.numpy as jnp
        import numpy as np
        E = 8
        TOPK = 2
        H = 256
        I = 256
        ISH = I * 2
        B, S = (2, 256)
        orig_shape = hidden_states.shape
        x = hidden_states.reshape(-1, orig_shape[-1])
        logits = x @ w_router
        top_logits, top_idx = jax.lax.top_k(logits, TOPK)
        scores = jax.nn.softmax(top_logits, axis=-1)
        flat_idx = top_idx.reshape(-1)
        sorted_idx = jnp.argsort(flat_idx)
        permuted = x[sorted_idx // TOPK]
        eid = flat_idx[sorted_idx]
        out_perm = jnp.zeros((permuted.shape[0], orig_shape[-1]), x.dtype)
        for e in range(E):
            m = (eid == e).astype(x.dtype)[:, None]
            h1 = permuted * m @ fc1_w[e]
            proj, gate = jnp.split(h1, 2, axis=-1)
            out_perm = out_perm + jax.nn.silu(proj) * gate @ fc2_w[e]
        unperm = jnp.zeros_like(out_perm).at[sorted_idx].set(out_perm)
        moe_out = (unperm.reshape(-1, TOPK, orig_shape[-1]) * scores[:, :, None]).sum(axis=1)
        moe_out = moe_out.reshape(orig_shape)
        shared = jax.nn.silu(hidden_states @ gate_w) * (hidden_states @ up_w) @ down_w
        return moe_out + shared
    x = x + jnp.tanh(g_xattn[0]) * _L0_xattn_ref(_layernorm(x, axis=-1), ctx_1024, ctx_1024, L0_xattn_Wq, L0_xattn_bq, L0_xattn_Wk, L0_xattn_bk, L0_xattn_Wv, L0_xattn_bv, L0_xattn_Wo, L0_xattn_bo)
    x = x + jnp.tanh(g_ffn[0]) * _L0_ffn_ref(_layernorm(x, axis=-1), L0_ffn_w_router, L0_ffn_fc1_w, L0_ffn_fc2_w, L0_ffn_gate_w, L0_ffn_up_w, L0_ffn_down_w)
    return x

_drawn_inputs = setup_inputs


def setup_inputs(seed=0):
    import zlib

    import numpy as np

    out = dict(_drawn_inputs(seed))
    spreads = {}
    factors = {'L0_xattn_bq': 8.0,
     'L0_xattn_bk': 8.0,
     'L0_xattn_bv': 8.0,
     'L0_xattn_bo': 7.774,
     'L0_ffn_w_router': 6.27,
     'L0_ffn_fc1_w': 5.414,
     'L0_ffn_fc2_w': 5.41,
     'L0_ffn_gate_w': 2.75,
     'L0_ffn_up_w': 2.721,
     'L0_ffn_down_w': 2.718}
    for name, (base, spread) in spreads.items():
        noise = np.random.default_rng([zlib.crc32(name.encode()), seed]).standard_normal(out[name].shape)
        drawn = base * np.exp(spread * noise) if base else spread * noise
        out[name] = jnp.asarray(drawn.astype(out[name].dtype))
    for name, factor in factors.items():
        out[name] = (out[name] * factor).astype(out[name].dtype)
    return out
```

```python
from contextlib import ExitStack

import concourse.bass as bass
from concourse import mybir

P = 128
ALU = mybir.AluOpType
ACT = mybir.ActivationFunctionType
AX = mybir.AxisListType
F32 = mybir.dt.float32
BF16 = mybir.dt.bfloat16
U32 = mybir.dt.uint32
I32 = mybir.dt.int32


def flamingo_layer(nc, x, ctxT, g_xattn, g_ffn, WqT, bq, WkT, bk, WvT, bv, WoT, bo,
                   w_router, fc1_w, fc2_w, gate_w, up_w, down_w, out):
    B, S, D = x.shape
    H = 16
    DK = D // H
    T = B * S
    NT = T // P
    TB = S // P
    DC = D // P
    E = fc1_w.shape[0]
    I2 = fc1_w.shape[2]
    IE = I2 // 2
    ISH = gate_w.shape[1]
    IC = ISH // P
    G = 4
    NG = H // G
    GROUPS = B * NG
    TERMS = 6
    Q_PART = [0, 1, 2, 0, 1, 0]
    K_PART = [0, 0, 0, 1, 1, 2]
    KS = TERMS * DK
    KM = KS + 2
    VW = 2 * DK
    SLOTS = (2 * T + E * (P - 1)) // P
    UN = 3
    assert SLOTS % UN == 0
    PASSES = SLOTS // UN
    EPS = 1e-5

    q_scr = nc.dram_tensor("q_parts", (B, 3, D, S), BF16, kind="Internal").ap()
    k_scr = nc.dram_tensor("k_parts", (B, 3, D, S), BF16, kind="Internal").ap()
    v_scr = nc.dram_tensor("v_rows", (B, TB, P, H * VW), F32, kind="Internal").ap()
    slot_x = nc.dram_tensor("slot_x", (SLOTS * P, D), F32, kind="Internal").ap()
    slot_y = nc.dram_tensor("slot_y", (SLOTS * P, D), F32, kind="Internal").ap()

    with ExitStack() as stack:
        def sb(name, shape, dt=F32):
            return stack.enter_context(nc.sbuf_tensor(name, shape, dt))

        def sem(name):
            return stack.enter_context(nc.semaphore(name))

        def sems(name, n):
            return [sem(f"{name}{i}") for i in range(n)]

        ident = sb("ident", [P, P])
        before = sb("before", [P, P])
        ones = sb("ones", [P, P])
        W = {n: sb(f"w_{n}", [P, DC, D]) for n in "qkvo"}
        wr = sb("wr", [P, DC, E])
        wgate = sb("wgate", [P, DC, ISH])
        wup = sb("wup", [P, DC, ISH])
        wdown = sb("wdown", [P, IC, D])
        fc2 = sb("fc2", [P, IE // P, E, D])
        bias_qk = sb("bias_qk", [P, 2, DC])
        bias_sc = sb("bias_sc", [P, 2, DC])
        bv_row = sb("bv_row", [P, D])
        bo_row = sb("bo_row", [P, D])
        gates = sb("gates", [P, 2])
        tg = sb("tg", [P, 2])
        X = sb("X", [P, NT, D])
        CH = sb("CH", [P, NT, D])
        ZERO = sb("ZERO", [P, D])
        stats = sb("stats", [P, NT, 6])
        mv = sb("mv", [P, NT, 2])
        var_eps = sb("var_eps", [P, NT])
        rstd = sb("rstd", [P, NT])
        minus_half = sb("minus_half", [P, NT])

        R1 = sb("R1", [P, 8192])
        R2 = sb("R2", [P, 8192])
        R3 = sb("R3", [P, 8192])
        R4 = sb("R4", [P, 3072])
        PS = stack.enter_context(nc.psum_tensor("PS", [P, 8, 512], F32))

        fc1 = R3[:, :].rearrange("p (c e n) -> p c e n", c=DC, e=E)
        XN = R2[:, 0:2048].rearrange("p (s t d) -> p s t d", s=2, t=TB)
        XNT = R2[:, 2048:4096].rearrange("p (s c n) -> p s c n", s=2, c=DC)
        CT = R2[:, 4096:6144].rearrange("p (s c n) -> p s c n", s=2, c=DC)
        QF = R2[:, 6144:8192].rearrange("p (j n) -> p j n", j=4)
        VA = R3[:, 0:4096].rearrange("p (s t w) -> p s t w", s=2, t=TB)
        RQ = R3[:, 4096:5120].rearrange("p (j n) -> p j n", j=2)
        QP = R3[:, 5120:8192].bitcast(BF16).rearrange("p (j a n) -> p j a n", j=4, a=3)
        QS = [R1[:, 1024 * g:1024 * (g + 1)].bitcast(BF16).rearrange("p (h n) -> p h n", h=G) for g in range(NG)]
        KST = [R1[:, 4096 + 1024 * g:4096 + 1024 * (g + 1)].bitcast(BF16).rearrange("p (h n) -> p h n", h=G)
               for g in range(NG)]
        PT = R2[:, :].rearrange("p (k h n) -> p k h n", k=TB, h=G)
        VG = [R4[:, 512 * g:512 * (g + 1)].rearrange("p (k w) -> p k w", k=TB) for g in range(NG)]
        OT = [R4[:, 2048 + 512 * i:2048 + 512 * (i + 1)] for i in range(2)]
        nmax = sb("nmax", [P, 2, G * TB])
        mparts = sb("mparts", [G * TB, 2, 2, P], BF16)
        rden = sb("rden", [P, 2, TB, G])
        CTT = R2[:, 0:2048].rearrange("p (s c n) -> p s c n", s=2, c=DC)
        AO = R2[:, 2048:4096].rearrange("p (s n) -> p s n", s=4)
        H2T = R1[:, 0:4096].rearrange("p (c n) -> p c n", c=DC)
        SG = R2[:, 4096:5120].rearrange("p (s n) -> p s n", s=2)
        HS = R1[:, 4096:8192].rearrange("p (s c n) -> p s c n", s=2, c=IC)
        XG = R4[:, 0:768].rearrange("p (s d) -> p s d", s=UN)
        XGT = R4[:, 768:1536].rearrange("p (s d) -> p s d", s=UN)
        HE = R4[:, 1536:2304].rearrange("p (s d) -> p s d", s=UN)
        HET = R4[:, 2304:3072].rearrange("p (s d) -> p s d", s=UN)
        SE = R2[:, 5120:5888].rearrange("p (s d) -> p s d", s=UN)
        YE = R2[:, 5888:6656].rearrange("p (s d) -> p s d", s=UN)
        NGA = 4
        GA = R1[:, 0:2 * NGA * D].rearrange("p (s k d) -> p s k d", s=NGA, k=2)
        FO = R1[:, 4096:4096 + NGA * D].rearrange("p (s d) -> p s d", s=NGA)

        LG = sb("LG", [P, NT, E])
        mx8 = sb("mx8", [P, NT, 8])
        ix8 = sb("ix8", [P, NT, 8], U32)
        ixf = sb("ixf", [P, NT, 2])
        io8 = sb("io8", [P, E])
        io16 = sb("io16", [P, NT])
        io40 = sb("io40", [P, SLOTS])
        OH = sb("OH", [P, 3, NT, E])
        CU = sb("CU", [P, 2, NT, E])
        cnt_gt = sb("cnt_gt", [P, E, NT])
        tl = sb("tl", [P, 4, E])
        pos_base = sb("pos_base", [P, NT, E])
        posf = sb("posf", [P, 2, NT])
        pos = sb("pos", [P, 2, NT], U32)
        ge = sb("ge", [P, SLOTS, E])
        eidf = sb("eidf", [P, SLOTS])
        eid = sb("eid", [1, SLOTS], I32)
        sc = sb("sc", [P, 4, NT])
        scg = sb("scg", [P, 2, NT])

        w_in = {n: sem(f"w_in_{n}") for n in ("q", "k", "v", "o", "router", "shared", "fc1", "fc2", "small")}
        x_in = sems("x_in", B)
        ct_in = sems("ct_in", 2)
        const_ready, consts = sem("const_ready"), sem("consts")
        scaled = sem("scaled")
        ln_stats, ln_mv, ln_ve, ln_rstd = sem("ln_stats"), sem("ln_mv"), sem("ln_ve"), sem("ln_rstd")
        xn_ready, xt_done, xnt_ready = sem("xn_ready"), sem("xt_done"), sem("xnt_ready")
        qk_done, v_done = sem("qk_done"), sem("v_done")
        qf_ready, q1_ready, qr_ready, q2_ready, q3_ready = (sem(n) for n in ("qf_ready", "q1_ready", "qr_ready", "q2_ready", "q3_ready"))
        qp_out, va_out = sems("qp_out", 4), sems("va_out", 2)
        va_ready = sem("va_ready")
        va_ones = sem("va_ones")

        ld_group = sems("ld_group", NG)
        kones = sem("kones")
        smax_done, max_ready = sem("smax_done"), sem("max_ready")
        mt_done, m1_ready, m2_ready = sem("mt_done"), sem("m1_ready"), sem("m2_ready")
        m_in = sems("m_in", 2)
        st_done, exp_done, pv_done, ot_ready = sem("st_done"), sem("exp_done"), sem("pv_done"), sem("ot_ready")
        ot_t, rden_ready, ctx_ready = sem("ot_t"), sem("rden_ready"), sem("ctx_ready")

        ct_t, ctt_ready, wo_done, ao_ready, x1_ready = (sem(n) for n in ("ct_t", "ctt_ready", "wo_done", "ao_ready", "x1_ready"))
        h2_ready, h2_t, h2t_ready, lg_done, lg_ready = (sem(n) for n in ("h2_ready", "h2_t", "h2t_ready", "lg_done", "lg_ready"))
        dve_route, route_pe, exp_sc = sem("dve_route"), sem("route_pe"), sem("exp_sc")
        zero_ready, zero_out, scattered = sem("zero_ready"), sem("zero_out"), sem("scattered")
        gu_done, silu_ready, hs_ready, down_done, base_ready = (sem(n) for n in ("gu_done", "silu_ready", "hs_ready", "down_done", "base_ready"))
        xg_in = sems("xg_in", UN)
        xg_t, xgt_ready, h1_done, se_ready, he_ready, he1 = (sem(n) for n in ("xg_t", "xgt_ready", "h1_done", "se_ready", "he_ready", "he1"))
        he_t, het_ready, y_done, y_ready = (sem(n) for n in ("he_t", "het_ready", "y_done", "y_ready"))
        y_out = sems("y_out", UN)
        ga_in = sems("ga_in", 2 * NGA)
        fo1, fo_ready = sem("fo1"), sem("fo_ready")
        fo_out = sems("fo_out", NGA)

        block = stack.enter_context(nc.Block())

        def wait(eng, s, n):
            if not isinstance(n, int) or n > 0:
                eng.wait_ge(s, n)

        def over_slots(eng, step):
            for it in range(2):
                for u in range(UN):
                    step(it, u, it == 0, False)
            with eng.Fori(2, PASSES - 1) as it:
                for u in range(UN):
                    step(it, u, False, False)
            for u in range(UN):
                step(PASSES - 1, u, False, True)

        def smax_schedule(i, kt):
            s = 4 * i + 6 + kt
            return s if s < GROUPS * G else None

        ROUTE_DIFF = 2 * NT + 2
        ROUTE_OH = ROUTE_DIFF + 3
        ROUTE_POS = ROUTE_OH + 27
        ROUTE_EID = ROUTE_POS + 3

        @block.sync
        def _(sp):
            for b in range(B):
                sp.dma_start(X[:, b * TB:(b + 1) * TB, :], x[b].rearrange("(t p) d -> p t d", p=P)).then_inc(x_in[b], 16)
                if b == 0:
                    sp.dma_start(W["q"][:, :, :], WqT.rearrange("(c p) n -> p c n", p=P)).then_inc(w_in["q"], 16)
                    sp.dma_start(W["k"][:, :, :], WkT.rearrange("(c p) n -> p c n", p=P)).then_inc(w_in["k"], 16)
                if b < 2:
                    sp.dma_start(CT[:, b, :, :], ctxT[:, b * S:(b + 1) * S].rearrange("(c p) n -> p c n", p=P))\
                      .then_inc(ct_in[b], 16)
                if b == 0:
                    sp.dma_start(W["v"][:, :, :], WvT.rearrange("(c p) n -> p c n", p=P)).then_inc(w_in["v"], 16)
            sp.dma_start(W["o"][:, :, :], WoT.rearrange("(c p) n -> p c n", p=P)).then_inc(w_in["o"], 16)
            sp.dma_start(wr[:, :, :], w_router.rearrange("(c p) n -> p c n", p=P)).then_inc(w_in["router"], 16)
            for t_, src in ((wgate, gate_w), (wup, up_w), (wdown, down_w)):
                sp.dma_start(t_[:, :, :], src.rearrange("(c p) n -> p c n", p=P)).then_inc(w_in["shared"], 16)
            for c in range(IE // P):
                sp.dma_start(fc2[:, c, :, :], fc2_w[:, c * P:(c + 1) * P, :].rearrange("e p n -> p e n")).then_inc(w_in["fc2"], 16)
            for b in range(B):
                if b >= 2:
                    sp.wait_ge(qk_done, 4 * (b - 1))
                    sp.wait_ge(v_done, 2 * (b - 1))
                    sp.dma_start(CT[:, b % 2, :, :], ctxT[:, b * S:(b + 1) * S].rearrange("(c p) n -> p c n", p=P))\
                      .then_inc(ct_in[b % 2], 16)
                for j in range(4):
                    dst = q_scr if j < 2 else k_scr
                    sp.wait_ge(q1_ready, 4 * b + j + 1)
                    sp.wait_ge(q2_ready, 4 * b + j + 1)
                    sp.wait_ge(q3_ready, 4 * b + j + 1)
                    sp.dma_start(dst[b, :, (j % 2) * P:(j % 2 + 1) * P, :].rearrange("a p n -> p a n"), QP[:, j, :, :])\
                      .then_inc(qp_out[j], 16)
                sp.wait_ge(va_ready, TB * (b + 1))
                sp.dma_start(v_scr[b].rearrange("t p w -> p t w"), VA[:, b % 2, :, :]).then_inc(va_out[b % 2], 16)
            for j in range(4):
                sp.wait_ge(qp_out[j], 16 * B)
            for s in range(2):
                sp.wait_ge(va_out[s], 16 * B // 2)
            sp.wait_ge(w_in["fc2"], 32)

            def load_group(i):
                b, g = divmod(i, NG)
                if i >= NG:
                    sp.wait_ge(pv_done, TB * (i - NG + 1))
                rows = slice(g * G * DK, (g + 1) * G * DK)
                for t in range(TERMS):
                    sp.dma_start(QS[g][t * DK:(t + 1) * DK, :, :],
                                 q_scr[b, Q_PART[t], rows, :].rearrange("(h d) n -> d h n", h=G)).then_inc(ld_group[g], 16)
                    sp.dma_start(KST[g][t * DK:(t + 1) * DK, :, :],
                                 k_scr[b, K_PART[t], rows, :].rearrange("(h d) n -> d h n", h=G)).then_inc(ld_group[g], 16)
                sp.dma_start(VG[g][:, :, :], v_scr[b, :, :, g * G * VW:(g + 1) * G * VW].rearrange("t p w -> p t w"))\
                  .then_inc(ld_group[g], 16)

            def load_max(i):
                for part, s in ((0, m1_ready), (1, m2_ready)):
                    sp.wait_ge(s, i + 1)
                    sp.dma_start(QS[i % NG][KS + part:KS + part + 1, :, :].rearrange("p h n -> p (h n)"),
                                 mparts[:, i % 2, part, :]).then_inc(m_in[i % 2], 16)

            for i in range(3):
                load_group(i)
            sp.dma_start(fc1[:, 0, :, :], fc1_w[:, 0:P, :].rearrange("e p n -> p e n")).then_inc(w_in["fc1"], 16)
            sp.dma_start(fc1[:, 1, :, :], fc1_w[:, P:2 * P, :].rearrange("e p n -> p e n")).then_inc(w_in["fc1"], 16)
            load_max(0)
            for i in range(GROUPS):
                if i + 3 < GROUPS:
                    load_group(i + 3)
                if i + 1 < GROUPS:
                    load_max(i + 1)
                if i == NG:
                    sp.wait_ge(zero_ready, 1)
                    sp.dma_start(slot_x.rearrange("(n p) d -> p n d", p=P), ZERO[:, :].unsqueeze(1).to_broadcast([P, SLOTS, D]))\
                      .then_inc(zero_out, 16)
            sp.wait_ge(scattered, 16 * 2 * NT)
            for u in range(UN):
                sp.dma_start(XG[:, u, :], slot_x[u * P:(u + 1) * P, :]).then_inc(xg_in[u], 16)

            def slot_dmas(it, u, first, last):
                j = it * UN + u
                if not last:
                    sp.wait_ge(xg_t, j + 1)
                    sp.dma_start(XG[:, u, :], slot_x[bass.ds((j + UN) * P, P), :]).then_inc(xg_in[u], 16)
                if not (first and u == 0):
                    before_u = (u - 1) % UN
                    sp.wait_ge(y_ready, j)
                    sp.dma_start(slot_y[bass.ds((j - 1) * P, P), :], YE[:, before_u, :]).then_inc(y_out[before_u], 16)

            over_slots(sp, slot_dmas)
            sp.wait_ge(y_ready, SLOTS)
            sp.dma_start(slot_y[(SLOTS - 1) * P:SLOTS * P, :], YE[:, UN - 1, :]).then_inc(y_out[UN - 1], 16)
            for t in range(NT):
                b, q = divmod(t, TB)
                sp.wait_ge(fo_ready, t + 1)
                sp.dma_start(out[b, q * P:(q + 1) * P, :], FO[:, t % NGA, :]).then_inc(fo_out[t % NGA], 16)
            for n in range(NGA):
                sp.wait_ge(fo_out[n], 16 * (NT // NGA))

        @block.gpsimd
        def _(pool):
            nc.gpsimd.memset(ident[:, :], 0.0).then_inc(const_ready, 1)
            nc.gpsimd.memset(before[:, :], 1.0).then_inc(const_ready, 1)
            nc.gpsimd.memset(ones[:, :], 1.0).then_inc(consts, 1)
            nc.gpsimd.memset(minus_half[:, :], -0.5).then_inc(consts, 1)
            nc.gpsimd.memset(ZERO[:, :], 0.0).then_inc(zero_ready, 1)
            pool.wait_ge(const_ready, 2)
            nc.gpsimd.affine_select(out=ident[:, :], in_=ident[:, :], compare_op=ALU.not_equal, fill=1.0, base=0,
                                    pattern=[[-1, P]], channel_multiplier=1).then_inc(consts, 1)
            nc.gpsimd.affine_select(out=before[:, :], in_=before[:, :], compare_op=ALU.is_gt, fill=0.0, base=0,
                                    pattern=[[1, P]], channel_multiplier=-1).then_inc(consts, 1)
            nc.gpsimd.iota(io8[:, :], [[1, E]], base=0, channel_multiplier=0,
                           allow_small_or_imprecise_dtypes=True).then_inc(consts, 1)
            nc.gpsimd.iota(io16[:, :], [[P, NT]], base=0, channel_multiplier=0,
                           allow_small_or_imprecise_dtypes=True).then_inc(consts, 1)
            nc.gpsimd.iota(io40[:, :], [[1, SLOTS]], base=0, channel_multiplier=0,
                           allow_small_or_imprecise_dtypes=True).then_inc(consts, 1)
            nc.gpsimd.memset(VA[:, :, :, :], 1.0).then_inc(va_ones, 1)
            for g in range(NG):
                pool.wait_ge(kones, g) if g else pool.wait_ge(va_ones, 1)
                nc.gpsimd.memset(KST[g][KS:KM, :, :], 1.0).then_inc(kones, 1)
            pool.wait_ge(kones, NG)
            for b in range(B):
                pool.wait_ge(ln_ve, b + 1)
                sl = slice(b * TB, (b + 1) * TB)
                nc.gpsimd.tensor_tensor(rstd[:, sl], var_eps[:, sl], minus_half[:, sl], ALU.pow).then_inc(ln_rstd, 1)
            for b in range(B):
                pool.wait_ge(ln_ve, B + b + 1)
                sl = slice(b * TB, (b + 1) * TB)
                nc.gpsimd.tensor_tensor(rstd[:, sl], var_eps[:, sl], minus_half[:, sl], ALU.pow).then_inc(ln_rstd, 1)
            pool.wait_ge(dve_route, ROUTE_POS)
            pool.wait_ge(zero_out, 16)
            for t in range(NT):
                for k in range(2):
                    nc.gpsimd.indirect_dma_start(slot_x, bass.IndirectOffsetOnAxis(ap=pos[:, k, t:t + 1], axis=0),
                                                 CH[:, t, :], None).then_inc(scattered, 16)
            for u in range(UN):
                pool.wait_ge(y_out[u], 16 * (SLOTS // UN))
            for t in range(NT):
                for k in range(2):
                    if t >= NGA:
                        pool.wait_ge(fo_ready, t - NGA + 1)
                    nc.gpsimd.indirect_dma_start(GA[:, t % NGA, k, :], None, slot_y,
                                                 bass.IndirectOffsetOnAxis(ap=pos[:, k, t:t + 1], axis=0))\
                        .then_inc(ga_in[2 * (t % NGA) + k], 16)

        @block.scalar
        def _(act):
            for n, (t_, src) in enumerate(((bias_qk[:, 0, :], bq), (bias_qk[:, 1, :], bk))):
                act.dma_start(t_, src).then_inc(w_in["small"], 16)
            for t_, src in ((bv_row, bv), (bo_row, bo)):
                act.dma_start(t_[:, :], src.partition_broadcast(P)).then_inc(w_in["small"], 16)
            for n, src in enumerate((g_xattn, g_ffn)):
                act.dma_start(gates[:, n:n + 1], src.partition_broadcast(P)).then_inc(w_in["small"], 16)
            act.wait_ge(w_in["small"], 96)
            nc.scalar.activation(tg[:, :], gates[:, :], ACT.Tanh).then_inc(scaled, 1)
            nc.scalar.activation(bias_sc[:, 0, :], bias_qk[:, 0, :], ACT.Copy, scale=0.25).then_inc(scaled, 1)
            nc.scalar.activation(bias_sc[:, 1, :], bias_qk[:, 1, :], ACT.Copy).then_inc(scaled, 1)
            act.wait_ge(scaled, 3)
            for b in range(B):
                s = b % 2
                act.wait_ge(xt_done, 2 * b + 1)
                if b >= 2:
                    act.wait_ge(qk_done, 4 * (b - 2) + 2)
                nc.scalar.copy(XNT[:, s, 0, :], PS[:, 0, :]).then_inc(xnt_ready, 1)
                for j in range(4):
                    act.wait_ge(qk_done, 4 * b + j + 1)
                    if b:
                        act.wait_ge(qr_ready, 4 * (b - 1) + j + 1)
                    bias = bias_sc[:, j // 2, j % 2:j % 2 + 1]
                    scale = 0.25 if j < 2 else 1.0
                    nc.scalar.activation(QF[:, j, :], PS[:, 2 + j, :], ACT.Identity, bias=bias, scale=scale).then_inc(qf_ready, 1)
                    if b:
                        act.wait_ge(qp_out[j], 16 * b)
                    nc.scalar.activation(QP[:, j, 0, :], PS[:, 2 + j, :], ACT.Identity, bias=bias, scale=scale).then_inc(q1_ready, 1)
            def m_first(i):
                act.wait_ge(mt_done, i + 1)
                if i >= 2:
                    act.wait_ge(m_in[i % 2], 32 * (i // 2))
                nc.scalar.copy(mparts[:, i % 2, 0, :], PS[0:G * TB, 7, 0:P]).then_inc(m1_ready, 1)

            def out_copy(i):
                act.wait_ge(pv_done, TB * (i + 1))
                if i >= 2:
                    act.wait_ge(ot_t, i - 1)
                nc.scalar.copy(OT[i % 2], PS[:, 6, :]).then_inc(ot_ready, 1)

            for i in range(GROUPS):
                if i == 0:
                    m_first(0)
                for kt in range(TB):
                    for a in range(2):
                        n = 8 * i + 2 * kt + a
                        act.wait_ge(st_done, n + 1)
                        if i:
                            act.wait_ge(pv_done, TB * (i - 1) + kt + 1)
                        nc.scalar.activation(PT[:, kt, 2 * a:2 * a + 2, :], PS[:, 2 * a:2 * a + 2, :], ACT.Exp)\
                            .then_inc(exp_done, 1)
                    if kt == 0 and i:
                        out_copy(i - 1)
                    if kt == 2 and i + 1 < GROUPS:
                        m_first(i + 1)
            out_copy(GROUPS - 1)
            for b in range(B):
                act.wait_ge(ct_t, 2 * b + 1)
                if b >= 2:
                    act.wait_ge(wo_done, 2 * (b - 1))
                nc.scalar.copy(CTT[:, b % 2, 0, :], PS[:, 0, :]).then_inc(ctt_ready, 1)
                act.wait_ge(h2_t, 2 * b + 1)
                nc.scalar.copy(H2T[:, 0, b * S:(b + 1) * S], PS[:, 4, :]).then_inc(h2t_ready, 1)
            act.wait_ge(dve_route, ROUTE_DIFF)
            nc.scalar.activation(sc[:, 1, :], sc[:, 0, :], ACT.Exp).then_inc(exp_sc, 1)
            for b in range(B):
                for c in range(IC):
                    n = IC * b + c
                    act.wait_ge(gu_done, n + 1)
                    if n >= 2:
                        act.wait_ge(hs_ready, n - 1)
                    nc.scalar.activation(SG[:, n % 2, :], PS[:, 2 * (n % 2), :], ACT.Silu).then_inc(silu_ready, 1)
            act.wait_ge(xg_t, 1)
            nc.scalar.copy(XGT[:, 0, :], PS[:, 0, 0:D]).then_inc(xgt_ready, 1)

            def slot_acts(it, u, first, last):
                j = it * UN + u
                act.wait_ge(h1_done, j + 1)
                if not first:
                    act.wait_ge(he_ready, j - UN + 1)
                nc.scalar.activation(SE[:, u, :], PS[:, 1 + u, 0:IE], ACT.Silu).then_inc(se_ready, 1)
                if not (last and u == UN - 1):
                    act.wait_ge(xg_t, j + 2)
                    nc.scalar.copy(XGT[:, (u + 1) % UN, :], PS[:, 0, 0:D]).then_inc(xgt_ready, 1)
                act.wait_ge(he_t, j + 1)
                nc.scalar.copy(HET[:, u, :], PS[:, 4, 0:IE]).then_inc(het_ready, 1)

            over_slots(act, slot_acts)

        @block.vector
        def _(dve):

            def layernorm(b, n0):
                sl = slice(b * TB, (b + 1) * TB)
                for t in range(TB):
                    nc.vector.bn_stats(stats[:, b * TB + t, :], X[:, b * TB + t, :]).then_inc(ln_stats, 1)
                dve.wait_ge(ln_stats, 4 * (n0 + b + 1))
                for t in range(TB):
                    nc.vector.bn_aggr(mv[:, b * TB + t, :], stats[:, b * TB + t, :]).then_inc(ln_mv, 1)
                dve.wait_ge(ln_mv, 4 * (n0 + b + 1))
                nc.vector.tensor_scalar(var_eps[:, sl], mv[:, sl, 1], EPS, None, ALU.add).then_inc(ln_ve, 1)

            def normalise(b, n0, dst, ready):
                dve.wait_ge(ln_rstd, n0 + b + 1)
                for t in range(TB):
                    tt = b * TB + t
                    nc.vector.tensor_scalar(dst(t), X[:, tt, :], mv[:, tt, 0:1], rstd[:, tt:tt + 1],
                                            ALU.subtract, ALU.mult).then_inc(ready, 1)

            dve.wait_ge(x_in[0], 16)
            layernorm(0, 0)
            for b in range(B):
                s = b % 2
                if b + 1 < B:
                    dve.wait_ge(x_in[b + 1], 16)
                    layernorm(b + 1, 0)
                if b >= 2:
                    dve.wait_ge(xt_done, 2 * (b - 1))
                normalise(b, 0, lambda t: XN[:, s, t, :], xn_ready)
                dve.wait_ge(xt_done, 2 * b + 2)
                if b >= 2:
                    dve.wait_ge(qk_done, 4 * (b - 2) + 2)
                nc.vector.tensor_copy(XNT[:, s, 1, :], PS[:, 1, :]).then_inc(xnt_ready, 1)
                dve.wait_ge(w_in["small"], 96)
                if b == 0:
                    dve.wait_ge(va_ones, 1)
                if b >= 2:
                    dve.wait_ge(va_out[s], 16 * (b // 2))
                for j in range(4):
                    n = 4 * b + j
                    dve.wait_ge(qf_ready, n + 1)
                    dve.wait_ge(q1_ready, n + 1)
                    if n >= 2:
                        dve.wait_ge(q3_ready, n - 1)
                    nc.vector.tensor_tensor(RQ[:, n % 2, :], QF[:, j, :], QP[:, j, 0, :], ALU.subtract).then_inc(qr_ready, 1)
                    dve.wait_ge(qr_ready, n + 1)
                    if b:
                        dve.wait_ge(qp_out[j], 16 * b)
                    nc.vector.tensor_copy(QP[:, j, 1, :], RQ[:, n % 2, :]).then_inc(q2_ready, 1)
                    dve.wait_ge(q2_ready, n + 1)
                    nc.vector.tensor_tensor(QP[:, j, 2, :], RQ[:, n % 2, :], QP[:, j, 1, :], ALU.subtract).then_inc(q3_ready, 1)
                for t in range(TB):
                    dve.wait_ge(v_done, 2 * b + t // 2 + 1)
                    nc.vector.tensor_tensor(
                        VA[:, s, t, :].rearrange("p (h w) -> p h w", w=VW)[:, :, 0:DK],
                        PS[:, 6 + t // 2, (t % 2) * D:(t % 2 + 1) * D].rearrange("p (h w) -> p h w", w=DK),
                        bv_row[:, :].rearrange("p (h w) -> p h w", w=DK), ALU.add).then_inc(va_ready, 1)

            def head_max(s):
                i, j = divmod(s, G)
                for qt in range(TB):
                    n = TB * s + qt
                    dve.wait_ge(smax_done, n + 1)
                    if n % 16 == 0 and i >= 2:
                        dve.wait_ge(mt_done, i - 1)
                    nc.vector.tensor_reduce(nmax[:, i % 2, j * TB + qt:j * TB + qt + 1], PS[:, 4 + n % 2, :], AX.X,
                                            ALU.max, negate=True).then_inc(max_ready, 1)

            def m_second(i):
                dve.wait_ge(m1_ready, i + 1)
                nc.vector.tensor_tensor(mparts[:, i % 2, 1, :], PS[0:G * TB, 7, 0:P], mparts[:, i % 2, 0, :],
                                        ALU.subtract).then_inc(m2_ready, 1)

            def head_out(i):
                b, g = divmod(i, NG)
                dve.wait_ge(ot_t, i + 1)
                o = PS[:, 7, :].rearrange("p (q h w) -> p q h w", q=TB, h=G)
                if i >= 2:
                    dve.wait_ge(ctx_ready, TB * (i - 1))
                nc.vector.reciprocal(rden[:, i % 2, :, :], o[:, :, :, DK]).then_inc(rden_ready, 1)
                dve.wait_ge(rden_ready, i + 1)
                for qt in range(TB):
                    nc.vector.tensor_tensor(
                        CH[:, b * TB + qt, g * G * DK:(g + 1) * G * DK].rearrange("p (h w) -> p h w", h=G),
                        o[:, qt, :, 0:DK], rden[:, i % 2, qt, :].unsqueeze(2).to_broadcast([P, G, DK]),
                        ALU.mult).then_inc(ctx_ready, 1)

            for s in range(6):
                head_max(s)
                if s == 4:
                    m_second(0)
            for i in range(GROUPS):
                for kt in range(TB):
                    s = smax_schedule(i, kt)
                    if s is not None:
                        head_max(s)
                    if kt == 1 and i:
                        head_out(i - 1)
                    if kt == 2 and i + 1 < GROUPS:
                        m_second(i + 1)
            head_out(GROUPS - 1)

            dve.wait_ge(w_in["small"], 96)
            dve.wait_ge(scaled, 3)
            for b in range(B):
                dve.wait_ge(ct_t, 2 * b + 2)
                if b >= 2:
                    dve.wait_ge(wo_done, 2 * (b - 1))
                nc.vector.tensor_copy(CTT[:, b % 2, 1, :], PS[:, 1, :]).then_inc(ctt_ready, 1)
                for h in range(2):
                    n = 2 * b + h
                    dve.wait_ge(wo_done, n + 1)
                    if n >= 4:
                        dve.wait_ge(x1_ready, n - 3)
                    tt = slice(b * TB + 2 * h, b * TB + 2 * h + 2)
                    nc.vector.tensor_tensor(AO[:, n % 4, :].rearrange("p (t d) -> p t d", t=2),
                                            PS[:, 2 + h, :].rearrange("p (t d) -> p t d", t=2),
                                            bo_row[:, :].unsqueeze(1).to_broadcast([P, 2, D]), ALU.add).then_inc(ao_ready, 1)
                    dve.wait_ge(ao_ready, n + 1)
                    nc.vector.scalar_tensor_tensor(out=X[:, tt, :], in0=AO[:, n % 4, :].rearrange("p (t d) -> p t d", t=2),
                                                   scalar=tg[:, 0:1], in1=X[:, tt, :], op0=ALU.mult, op1=ALU.add)\
                        .then_inc(x1_ready, 1)
                dve.wait_ge(x1_ready, 2 * b + 2)
                layernorm(b, B)
                normalise(b, B, lambda t: CH[:, b * TB + t, :], h2_ready)
                dve.wait_ge(h2_t, 2 * b + 2)
                nc.vector.tensor_copy(H2T[:, 1, b * S:(b + 1) * S], PS[:, 5, :]).then_inc(h2t_ready, 1)
                dve.wait_ge(lg_done, b + 1)
                nc.vector.tensor_copy(LG[:, b * TB:(b + 1) * TB, :],
                                      PS[:, 6, 0:TB * E].rearrange("p (t e) -> p t e", t=TB)).then_inc(lg_ready, 1)

            chain = [0]

            def step(ins):
                chain[0] += 1
                ins.then_inc(dve_route, 1)
                dve.wait_ge(dve_route, chain[0])

            def many(instructions):
                for ins in instructions:
                    chain[0] += 1
                    ins.then_inc(dve_route, 1)
                dve.wait_ge(dve_route, chain[0])

            dve.wait_ge(lg_ready, B)
            dve.wait_ge(consts, 7)
            many(nc.vector.max(mx8[:, t, :], LG[:, t, :]) for t in range(NT))
            many(nc.vector.max_index(ix8[:, t, :], mx8[:, t, :], LG[:, t, :]) for t in range(NT))
            step(nc.vector.tensor_copy(ixf[:, :, :], ix8[:, :, 0:2]))
            step(nc.vector.tensor_tensor(sc[:, 0, :], mx8[:, :, 1], mx8[:, :, 0], ALU.subtract))
            assert chain[0] == ROUTE_DIFF
            for k in range(2):
                step(nc.vector.tensor_tensor(OH[:, k, :, :], io8[:, :].unsqueeze(1).to_broadcast([P, NT, E]),
                                             ixf[:, :, k].unsqueeze(2).to_broadcast([P, NT, E]), ALU.is_equal))
            step(nc.vector.tensor_tensor(OH[:, 2, :, :], OH[:, 0, :, :], OH[:, 1, :, :], ALU.add))
            assert chain[0] == ROUTE_OH
            dve.wait_ge(route_pe, 2)
            tot = PS[:, 5, 0:NT * E].rearrange("p (t e) -> p t e", t=NT)
            rank = PS[:, 4, 0:NT * E].rearrange("p (t e) -> p t e", t=NT)
            step(nc.vector.tensor_copy(CU[:, 0, :, :], tot))
            a = 0
            for d in (1, 2, 4, 8):
                many([nc.vector.tensor_copy(CU[:, 1 - a, 0:d, :], CU[:, a, 0:d, :]),
                      nc.vector.tensor_tensor(CU[:, 1 - a, d:NT, :], CU[:, a, d:NT, :], CU[:, a, 0:NT - d, :], ALU.add)])
                a = 1 - a
            step(nc.vector.tensor_tensor(cnt_gt[:, :, :], CU[:, a, NT - 1, :].unsqueeze(2).to_broadcast([P, E, NT]),
                                         io16[:, :].unsqueeze(1).to_broadcast([P, E, NT]), ALU.is_gt))
            step(nc.vector.tensor_reduce(tl[:, 0, :], cnt_gt[:, :, :], AX.X, ALU.add))
            src = 0
            for n, d in enumerate((1, 2, 4)):
                to = n + 1
                many([nc.vector.tensor_copy(tl[:, to, 0:d], tl[:, src, 0:d]),
                      nc.vector.tensor_tensor(tl[:, to, d:E], tl[:, src, d:E], tl[:, src, 0:E - d], ALU.add)])
                src = to
            step(nc.vector.tensor_tensor(pos_base[:, :, :], CU[:, a, :, :], rank, ALU.add))
            step(nc.vector.tensor_tensor(CU[:, 1 - a, :, :], pos_base[:, :, :], tot, ALU.subtract))
            step(nc.vector.tensor_tensor(tl[:, 1, :], tl[:, 3, :], tl[:, 0, :], ALU.subtract))
            step(nc.vector.tensor_scalar(tl[:, 2, :], tl[:, 1, :], float(P), None, ALU.mult))
            step(nc.vector.tensor_tensor(pos_base[:, :, :], CU[:, 1 - a, :, :],
                                         tl[:, 2, :].unsqueeze(1).to_broadcast([P, NT, E]), ALU.add))
            for k in range(2):
                step(nc.vector.tensor_tensor(CU[:, k, :, :], OH[:, k, :, :], pos_base[:, :, :], ALU.mult))
                step(nc.vector.tensor_reduce(posf[:, k, :], CU[:, k, :, :], AX.X, ALU.add))
            step(nc.vector.tensor_copy(pos[:, :, :], posf[:, :, :]))
            assert chain[0] == ROUTE_POS, chain[0]
            step(nc.vector.tensor_tensor(ge[:, :, :], io40[:, :].unsqueeze(2).to_broadcast([P, SLOTS, E]),
                                         tl[:, 3, :].unsqueeze(1).to_broadcast([P, SLOTS, E]), ALU.is_ge))
            step(nc.vector.tensor_reduce(eidf[:, :], ge[:, :, :], AX.X, ALU.add))
            step(nc.vector.tensor_scalar(eid[:, :], eidf[0:1, :], float(E - 1), None, ALU.min))
            assert chain[0] == ROUTE_EID, chain[0]
            dve.wait_ge(exp_sc, 1)
            step(nc.vector.tensor_scalar(sc[:, 2, :], sc[:, 1, :], 1.0, None, ALU.add))
            step(nc.vector.reciprocal(sc[:, 3, :], sc[:, 2, :]))
            step(nc.vector.tensor_tensor(sc[:, 0, :], sc[:, 1, :], sc[:, 3, :], ALU.mult))
            step(nc.vector.tensor_scalar(scg[:, 0, :], sc[:, 3, :], tg[:, 1:2], None, ALU.mult))
            step(nc.vector.tensor_scalar(scg[:, 1, :], sc[:, 0, :], tg[:, 1:2], None, ALU.mult))

            for b in range(B):
                for c in range(IC):
                    n = IC * b + c
                    dve.wait_ge(silu_ready, n + 1)
                    if b >= 2:
                        dve.wait_ge(down_done, 2 * (b - 1))
                    nc.vector.tensor_tensor(HS[:, b % 2, c, :], SG[:, n % 2, :], PS[:, 2 * (n % 2) + 1, :], ALU.mult)\
                        .then_inc(hs_ready, 1)
                for h in range(2):
                    dve.wait_ge(down_done, 2 * b + h + 1)
                    tt = slice(b * TB + 2 * h, b * TB + 2 * h + 2)
                    nc.vector.scalar_tensor_tensor(out=X[:, tt, :], in0=PS[:, 6 + h, :].rearrange("p (t d) -> p t d", t=2),
                                                   scalar=tg[:, 1:2], in1=X[:, tt, :], op0=ALU.mult, op1=ALU.add)\
                        .then_inc(base_ready, 1)
            def slot_result(it, u, first):
                dve.wait_ge(y_done, it * UN + u + 1)
                if not first:
                    dve.wait_ge(y_out[u], it * 16)
                nc.vector.tensor_copy(YE[:, u, :], PS[:, 5 + u, 0:D]).then_inc(y_ready, 1)

            def slot_products(it, u, first, last):
                dve.wait_ge(se_ready, it * UN + u + 1)
                if not first:
                    dve.wait_ge(he_t, (it - 1) * UN + u + 1)
                nc.vector.tensor_tensor(HE[:, u, :], SE[:, u, :], PS[:, 1 + u, IE:I2], ALU.mult).then_inc(he_ready, 1)
                if u:
                    slot_result(it, u - 1, first)
                elif not first:
                    slot_result(it - 1, UN - 1, isinstance(it, int) and it == 1)

            over_slots(dve, slot_products)
            slot_result(PASSES - 1, UN - 1, False)
            for t in range(NT):
                n = t % NGA
                dve.wait_ge(ga_in[2 * n], 16 * (t // NGA + 1))
                dve.wait_ge(ga_in[2 * n + 1], 16 * (t // NGA + 1))
                dve.wait_ge(base_ready, 2 * B)
                nc.vector.scalar_tensor_tensor(out=X[:, t, :], in0=GA[:, n, 0, :], scalar=scg[:, 0, t:t + 1],
                                               in1=X[:, t, :], op0=ALU.mult, op1=ALU.add).then_inc(fo1, 1)
                dve.wait_ge(fo1, t + 1)
                if t >= NGA:
                    dve.wait_ge(fo_out[n], 16 * (t // NGA))
                nc.vector.scalar_tensor_tensor(out=FO[:, n, :], in0=GA[:, n, 1, :], scalar=scg[:, 1, t:t + 1],
                                               in1=X[:, t, :], op0=ALU.mult, op1=ALU.add).then_inc(fo_ready, 1)

        @block.tensor
        def _(pe):
            mm = nc.tensor.matmul
            pe.wait_ge(consts, 3)
            for b in range(B):
                s = b % 2
                for c in range(DC):
                    pe.wait_ge(xn_ready, TB * (b + 1))
                    if b:
                        pe.wait_ge(xnt_ready, 2 * b)
                    for t in range(TB):
                        last = nc.tensor.transpose(PS[:, c, t * P:(t + 1) * P], XN[:, s, t, c * P:(c + 1) * P], ident[:, :])
                    last.then_inc(xt_done, 1)
                for n in ("k", "v"):
                    pe.wait_ge(w_in[n], 16)
                pe.wait_ge(w_in["q"], 16)
                pe.wait_ge(ct_in[s], 16 * (b // 2 + 1))
                for t in range(TB):
                    if b:
                        pe.wait_ge(va_ready, TB * b)
                    for c in range(DC):
                        last = mm(PS[:, 6 + t // 2, (t % 2) * D:(t % 2 + 1) * D], CT[:, s, c, t * P:(t + 1) * P],
                                  W["v"][:, c, :], start=(c == 0), stop=(c == DC - 1))
                    if t % 2:
                        last.then_inc(v_done, 1)
                for j in (0, 1, 2, 3):
                    if j == 0:
                        pe.wait_ge(xnt_ready, 2 * (b + 1))
                    if b:
                        pe.wait_ge(q1_ready, 4 * (b - 1) + j + 1)
                    w, src = (W["q"], XNT) if j < 2 else (W["k"], CT)
                    for c in range(DC):
                        last = mm(PS[:, 2 + j, :], w[:, c, (j % 2) * P:(j % 2 + 1) * P], src[:, s, c, :],
                                  start=(c == 0), stop=(c == DC - 1))
                    last.then_inc(qk_done, 1)

            def scores_for_max(s):
                i, j = divmod(s, G)
                b, g = divmod(i, NG)
                if j == 0:
                    pe.wait_ge(ld_group[g], 16 * (2 * TERMS + 1) * (b + 1))
                for qt in range(TB):
                    n = TB * s + qt
                    if n >= 2:
                        pe.wait_ge(max_ready, n - 1)
                    else:
                        pe.wait_ge(q1_ready, 4 * B)
                    mm(PS[:, 4 + n % 2, :], QS[g][0:KS, j, qt * P:(qt + 1) * P], KST[g][0:KS, j, :],
                       start=True, stop=True).then_inc(smax_done, 1)

            def max_transpose(i):
                pe.wait_ge(max_ready, TB * G * (i + 1))
                if i == 0:
                    pe.wait_ge(va_ready, TB * B)
                if i >= 2:
                    pe.wait_ge(ctx_ready, TB * (i - 1))
                nc.tensor.transpose(PS[0:G * TB, 7, 0:P], nmax[:, i % 2, :], ident[:, :]).then_inc(mt_done, 1)

            def values(i, kt):
                g = i % NG
                pe.wait_ge(exp_done, 8 * i + 2 * kt + 2)
                if kt == 0 and i:
                    pe.wait_ge(ot_ready, i)
                if kt == 0 and i == 0:
                    pe.wait_ge(va_ready, TB * B)
                for j in range(G):
                    last = mm(PS[32 * j:32 * j + VW, 6, :], VG[g][:, kt, j * VW:(j + 1) * VW], PT[:, kt, j, :],
                              start=(kt == 0), stop=(kt == TB - 1), tile_position=(0, 32 * j))
                last.then_inc(pv_done, 1)

            def out_transpose(i):
                pe.wait_ge(ot_ready, i + 1)
                pe.wait_ge(m2_ready, min(i + 2, GROUPS))
                wait(pe, ctx_ready, TB * i)
                for qt in range(TB):
                    last = nc.tensor.transpose(PS[:, 7, qt * P:(qt + 1) * P], OT[i % 2][:, qt * P:(qt + 1) * P], ident[:, :])
                last.then_inc(ot_t, 1)

            for s in range(6):
                scores_for_max(s)
                if s == 4:
                    max_transpose(0)
            for i in range(GROUPS):
                b, g = divmod(i, NG)
                pe.wait_ge(m_in[i % 2], 32 * (i // 2 + 1))
                if i < NG:
                    pe.wait_ge(kones, g + 1)
                for kt in range(TB):
                    for a in range(2):
                        n = 8 * i + 2 * kt + a
                        if n >= 2:
                            pe.wait_ge(exp_done, n - 1)
                        for j in (2 * a, 2 * a + 1):
                            last = mm(PS[:, j, :], KST[g][0:KM, j, kt * P:(kt + 1) * P], QS[g][0:KM, j, :],
                                      start=True, stop=True)
                        last.then_inc(st_done, 1)
                    s = smax_schedule(i, kt)
                    if s is not None:
                        scores_for_max(s)
                    if kt:
                        values(i, kt - 1)
                    elif i:
                        values(i - 1, TB - 1)
                    if kt == 1 and i:
                        out_transpose(i - 1)
                    if kt == 2 and i + 1 < GROUPS:
                        max_transpose(i + 1)
            values(GROUPS - 1, TB - 1)
            out_transpose(GROUPS - 1)

            for b in range(B):
                for c in range(DC):
                    pe.wait_ge(ctx_ready, TB * NG * (b + 1))
                    if b == 0:
                        pe.wait_ge(exp_done, 8 * GROUPS)
                    else:
                        pe.wait_ge(ctt_ready, 2 * b)
                    for t in range(TB):
                        last = nc.tensor.transpose(PS[:, c, t * P:(t + 1) * P], CH[:, b * TB + t, c * P:(c + 1) * P], ident[:, :])
                    last.then_inc(ct_t, 1)
                pe.wait_ge(w_in["o"], 16)
                pe.wait_ge(ctt_ready, 2 * (b + 1))
                for t in range(TB):
                    if b:
                        pe.wait_ge(ao_ready, 2 * (b - 1) + t // 2 + 1)
                    for c in range(DC):
                        last = mm(PS[:, 2 + t // 2, (t % 2) * D:(t % 2 + 1) * D], CTT[:, b % 2, c, t * P:(t + 1) * P],
                                  W["o"][:, c, :], start=(c == 0), stop=(c == DC - 1))
                    if t % 2:
                        last.then_inc(wo_done, 1)
                for c in range(DC):
                    pe.wait_ge(h2_ready, TB * (b + 1))
                    if b:
                        pe.wait_ge(h2t_ready, 2 * b)
                    for t in range(TB):
                        last = nc.tensor.transpose(PS[:, 4 + c, t * P:(t + 1) * P], CH[:, b * TB + t, c * P:(c + 1) * P], ident[:, :])
                    last.then_inc(h2_t, 1)
                pe.wait_ge(w_in["router"], 16)
                pe.wait_ge(h2t_ready, 2 * (b + 1))
                if b:
                    pe.wait_ge(lg_ready, b)
                for t in range(TB):
                    for c in range(DC):
                        last = mm(PS[:, 6, t * E:(t + 1) * E], H2T[:, c, b * S + t * P:b * S + (t + 1) * P], wr[:, c, :],
                                  start=(c == 0), stop=(c == DC - 1))
                last.then_inc(lg_done, 1)
            pe.wait_ge(dve_route, ROUTE_OH)
            pe.wait_ge(consts, 7)
            choice = OH[:, 2, :, :].rearrange("p t e -> p (t e)")
            mm(PS[:, 4, 0:NT * E], before[:, :], choice, start=True, stop=True).then_inc(route_pe, 1)
            mm(PS[:, 5, 0:NT * E], ones[:, :], choice, start=True, stop=True).then_inc(route_pe, 1)

            pe.wait_ge(w_in["shared"], 48)
            for b in range(B):
                for c in range(IC):
                    n = IC * b + c
                    if n >= 2:
                        pe.wait_ge(hs_ready, n - 1)
                    for k, w in enumerate((wgate, wup)):
                        for d in range(DC):
                            last = mm(PS[:, 2 * (n % 2) + k, :], w[:, d, c * P:(c + 1) * P], H2T[:, d, b * S:(b + 1) * S],
                                      start=(d == 0), stop=(d == DC - 1))
                    last.then_inc(gu_done, 1)
                pe.wait_ge(hs_ready, IC * (b + 1))
                for t in range(TB):
                    if b:
                        pe.wait_ge(base_ready, 2 * (b - 1) + t // 2 + 1)
                    for c in range(IC):
                        last = mm(PS[:, 6 + t // 2, (t % 2) * D:(t % 2 + 1) * D], HS[:, b % 2, c, t * P:(t + 1) * P],
                                  wdown[:, c, :], start=(c == 0), stop=(c == IC - 1))
                    if t % 2:
                        last.then_inc(down_done, 1)

            pe.wait_ge(w_in["fc1"], 32)
            pe.wait_ge(w_in["fc2"], 32)
            pe.wait_ge(dve_route, ROUTE_EID)
            pe.wait_ge(base_ready, 2 * B)
            expert = [pe.alloc_register(f"expert{k}") for k in range(2)]

            def expert_of(k, j):
                pe.reg_load(expert[k], eid[0:1, bass.ds(j, 1)])
                return bass.ds(pe.snap(expert[k], min_val=0, max_val=E - 1), 1)

            def transpose_rows(it, u, first):
                pe.wait_ge(xg_in[u], (it + 1) * 16)
                if not (first and u == 0):
                    pe.wait_ge(xgt_ready, it * UN + u)
                for c in range(DC):
                    last = nc.tensor.transpose(PS[:, 0, c * P:(c + 1) * P], XG[:, u, c * P:(c + 1) * P], ident[:, :])
                last.then_inc(xg_t, 1)

            def second_product(it, u, first):
                e = expert_of(1, it * UN + u)
                pe.wait_ge(het_ready, it * UN + u + 1)
                if not first:
                    pe.wait_ge(y_ready, (it - 1) * UN + u + 1)
                for c in range(IE // P):
                    last = mm(PS[:, 5 + u, 0:D], HET[:, u, c * P:(c + 1) * P], fc2[:, c, e, :],
                              start=(c == 0), stop=(c == IE // P - 1))
                last.then_inc(y_done, 1)

            def slot_matmuls(it, u, first, last):
                j = it * UN + u
                e = expert_of(0, j)
                pe.wait_ge(xgt_ready, j + 1)
                if not first:
                    pe.wait_ge(he_ready, (it - 1) * UN + u + 1)
                for c in range(DC):
                    last_mm = mm(PS[:, 1 + u, :], XGT[:, u, c * P:(c + 1) * P], fc1[:, c, e, :],
                                 start=(c == 0), stop=(c == DC - 1))
                last_mm.then_inc(h1_done, 1)
                if u < UN - 1:
                    transpose_rows(it, u + 1, first)
                elif not last:
                    transpose_rows(it + 1, 0, False)
                if u:
                    second_product(it, u - 1, first)
                elif not first:
                    second_product(it - 1, UN - 1, isinstance(it, int) and it == 1)
                pe.wait_ge(he_ready, j + 1)
                if not (first and u == 0):
                    pe.wait_ge(het_ready, j)
                for c in range(IE // P):
                    last_mm = nc.tensor.transpose(PS[:, 4, c * P:(c + 1) * P], HE[:, u, c * P:(c + 1) * P], ident[:, :])
                last_mm.then_inc(he_t, 1)

            transpose_rows(0, 0, True)
            over_slots(pe, slot_matmuls)
            second_product(PASSES - 1, UN - 1, False)


_INS = ['x', 'ctx_1024T', 'g_xattn', 'g_ffn', 'WqT', 'bq', 'WkT', 'bk', 'WvT', 'bv', 'WoT', 'bo',
        'w_router', 'fc1_w', 'fc2_w', 'gate_w', 'up_w', 'down_w']


def kernel(**inputs):
    import numpy as _np
    import concourse.bacc as _bacc
    from concourse.bass_utils import run_bass_kernel_spmd as _run

    a = {k: _np.asarray(v) for k, v in inputs.items()}
    B, S, D = a['x'].shape
    laid = [
        a['x'],
        a['ctx_1024'].reshape(B * S, D).T,
        a['g_xattn'], a['g_ffn'],
    ]
    for n in 'qkvo':
        b = a[f'L0_xattn_b{n}']
        laid += [a[f'L0_xattn_W{n}'].T, b.reshape(-1, P).T if n in 'qk' else b]
    laid += [a[f'L0_ffn_{n}'] for n in ('w_router', 'fc1_w', 'fc2_w', 'gate_w', 'up_w', 'down_w')]

    nc = _bacc.Bacc("TRN2", target_bir_lowering=False, num_devices=1)
    arrays, args = {}, []
    for name, v in zip(_INS, laid):
        v = _np.ascontiguousarray(v)
        arrays[f"in_{name}_dram"] = v
        args.append(nc.dram_tensor(f"in_{name}_dram", v.shape, mybir.dt.from_np(v.dtype), kind="ExternalInput").ap())
    args.append(nc.dram_tensor("out_dram", (B, S, D), F32, kind="ExternalOutput").ap())
    flamingo_layer(nc, *args)
    r = _run(nc, [arrays], core_ids=[0])
    return r.results[0]["out_dram"]
```

```python
from contextlib import ExitStack

import concourse.bass as bass
from concourse import mybir

P = 128
ALU = mybir.AluOpType
ACT = mybir.ActivationFunctionType
AX = mybir.AxisListType
F32 = mybir.dt.float32
BF16 = mybir.dt.bfloat16
U32 = mybir.dt.uint32
I32 = mybir.dt.int32


def flamingo_layer(nc, x, ctxT, g_xattn, g_ffn, WqT, bq, WkT, bk, WvT, bv, WoT, bo,
                   w_router, fc1_w, fc2_w, gate_w, up_w, down_w, out):
    B, S, D = x.shape
    H = 16
    DK = D // H
    T = B * S
    NT = T // P
    TB = S // P
    DC = D // P
    E = fc1_w.shape[0]
    I2 = fc1_w.shape[2]
    IE = I2 // 2
    ISH = gate_w.shape[1]
    IC = ISH // P
    G = 4
    NG = H // G
    GROUPS = B * NG
    TERMS = 6
    Q_PART = [0, 1, 2, 0, 1, 0]
    K_PART = [0, 0, 0, 1, 1, 2]
    KS = TERMS * DK
    KM = KS + 2
    VW = 2 * DK
    SLOTS = (2 * T + E * (P - 1)) // P
    UN = 3
    assert SLOTS % UN == 0
    PASSES = SLOTS // UN
    EPS = 1e-5

    q_scr = nc.dram_tensor("q_parts", (B, 3, D, S), BF16, kind="Internal").ap()
    k_scr = nc.dram_tensor("k_parts", (B, 3, D, S), BF16, kind="Internal").ap()
    v_scr = nc.dram_tensor("v_rows", (B, TB, P, H * VW), F32, kind="Internal").ap()
    slot_x = nc.dram_tensor("slot_x", (SLOTS * P, D), F32, kind="Internal").ap()
    slot_y = nc.dram_tensor("slot_y", (SLOTS * P, D), F32, kind="Internal").ap()

    with ExitStack() as stack:
        def sb(name, shape, dt=F32):
            return stack.enter_context(nc.sbuf_tensor(name, shape, dt))

        def sem(name):
            return stack.enter_context(nc.semaphore(name))

        def sems(name, n):
            return [sem(f"{name}{i}") for i in range(n)]

        ident = sb("ident", [P, P])
        before = sb("before", [P, P])
        ones = sb("ones", [P, P])
        W = {n: sb(f"w_{n}", [P, DC, D]) for n in "qkvo"}
        wr = sb("wr", [P, DC, E])
        wgate = sb("wgate", [P, DC, ISH])
        wup = sb("wup", [P, DC, ISH])
        wdown = sb("wdown", [P, IC, D])
        fc2 = sb("fc2", [P, IE // P, E, D])
        bias_qk = sb("bias_qk", [P, 2, DC])
        bias_sc = sb("bias_sc", [P, 2, DC])
        bv_row = sb("bv_row", [P, D])
        bo_row = sb("bo_row", [P, D])
        gates = sb("gates", [P, 2])
        tg = sb("tg", [P, 2])
        X = sb("X", [P, NT, D])
        CH = sb("CH", [P, NT, D])
        ZERO = sb("ZERO", [P, D])
        stats = sb("stats", [P, NT, 6])
        mv = sb("mv", [P, NT, 2])
        var_eps = sb("var_eps", [P, NT])
        rstd = sb("rstd", [P, NT])
        minus_half = sb("minus_half", [P, NT])

        R1 = sb("R1", [P, 8192])
        R2 = sb("R2", [P, 8192])
        R3 = sb("R3", [P, 8192])
        R4 = sb("R4", [P, 3072])
        PS = stack.enter_context(nc.psum_tensor("PS", [P, 8, 512], F32))

        fc1 = R3[:, :].rearrange("p (c e n) -> p c e n", c=DC, e=E)
        XN = R2[:, 0:2048].rearrange("p (s t d) -> p s t d", s=2, t=TB)
        XNT = R2[:, 2048:4096].rearrange("p (s c n) -> p s c n", s=2, c=DC)
        CT = R2[:, 4096:6144].rearrange("p (s c n) -> p s c n", s=2, c=DC)
        QF = R2[:, 6144:8192].rearrange("p (j n) -> p j n", j=4)
        VA = R3[:, 0:4096].rearrange("p (s t w) -> p s t w", s=2, t=TB)
        RQ = R3[:, 4096:5120].rearrange("p (j n) -> p j n", j=2)
        QP = R3[:, 5120:8192].bitcast(BF16).rearrange("p (j a n) -> p j a n", j=4, a=3)
        QS = [R1[:, 1024 * g:1024 * (g + 1)].bitcast(BF16).rearrange("p (h n) -> p h n", h=G) for g in range(NG)]
        KST = [R1[:, 4096 + 1024 * g:4096 + 1024 * (g + 1)].bitcast(BF16).rearrange("p (h n) -> p h n", h=G)
               for g in range(NG)]
        PT = R2[:, :].rearrange("p (k h n) -> p k h n", k=TB, h=G)
        VG = [R4[:, 512 * g:512 * (g + 1)].rearrange("p (k w) -> p k w", k=TB) for g in range(NG)]
        OT = [R4[:, 2048 + 512 * i:2048 + 512 * (i + 1)] for i in range(2)]
        nmax = sb("nmax", [P, 2, G * TB])
        mparts = sb("mparts", [G * TB, 2, 2, P], BF16)
        rden = sb("rden", [P, 2, TB, G])
        CTT = R2[:, 0:2048].rearrange("p (s c n) -> p s c n", s=2, c=DC)
        AO = R2[:, 2048:4096].rearrange("p (s n) -> p s n", s=4)
        H2T = R1[:, 0:4096].rearrange("p (c n) -> p c n", c=DC)
        SG = R2[:, 4096:5120].rearrange("p (s n) -> p s n", s=2)
        HS = R1[:, 4096:8192].rearrange("p (s c n) -> p s c n", s=2, c=IC)
        XG = R4[:, 0:768].rearrange("p (s d) -> p s d", s=UN)
        XGT = R4[:, 768:1536].rearrange("p (s d) -> p s d", s=UN)
        HE = R4[:, 1536:2304].rearrange("p (s d) -> p s d", s=UN)
        HET = R4[:, 2304:3072].rearrange("p (s d) -> p s d", s=UN)
        SE = R2[:, 5120:5888].rearrange("p (s d) -> p s d", s=UN)
        YE = R2[:, 5888:6656].rearrange("p (s d) -> p s d", s=UN)
        NGA = 8
        GA = R3[:, 0:2 * NGA * D].rearrange("p (s k d) -> p s k d", s=NGA, k=2)
        FO = R3[:, 4096:4096 + NGA * D].rearrange("p (s d) -> p s d", s=NGA)

        LG = sb("LG", [P, NT, E])
        mx8 = sb("mx8", [P, NT, 8])
        ix8 = sb("ix8", [P, NT, 8], U32)
        ixf = sb("ixf", [P, NT, 2])
        io8 = sb("io8", [P, E])
        io16 = sb("io16", [P, NT])
        io40 = sb("io40", [P, SLOTS])
        OH = sb("OH", [P, 3, NT, E])
        CU = sb("CU", [P, 2, NT, E])
        cnt_gt = sb("cnt_gt", [P, E, NT])
        tl = sb("tl", [P, 4, E])
        pos_base = sb("pos_base", [P, NT, E])
        posf = sb("posf", [P, 2, NT])
        pos = sb("pos", [P, 2, NT], U32)
        ge = sb("ge", [P, SLOTS, E])
        eidf = sb("eidf", [P, SLOTS])
        eid = sb("eid", [1, SLOTS], I32)
        sc = sb("sc", [P, 4, NT])
        scg = sb("scg", [P, 2, NT])

        w_in = {n: sem(f"w_in_{n}") for n in ("q", "k", "v", "o", "router", "shared", "fc1", "fc2", "small")}
        x_in = sems("x_in", B)
        ct_in = sems("ct_in", 2)
        const_ready, consts = sem("const_ready"), sem("consts")
        scaled = sem("scaled")
        ln_stats, ln_mv, ln_ve, ln_rstd = sem("ln_stats"), sem("ln_mv"), sem("ln_ve"), sem("ln_rstd")
        xn_ready, xt_done, xnt_ready = sem("xn_ready"), sem("xt_done"), sem("xnt_ready")
        qk_done, v_done = sem("qk_done"), sem("v_done")
        qf_ready, q1_ready, qr_ready, q2_ready, q3_ready = (sem(n) for n in ("qf_ready", "q1_ready", "qr_ready", "q2_ready", "q3_ready"))
        qp_out, va_out = sems("qp_out", 4), sems("va_out", 2)
        va_ready = sem("va_ready")
        va_ones = sem("va_ones")

        ld_group = sems("ld_group", NG)
        kones = sem("kones")
        smax_done, max_ready = sem("smax_done"), sem("max_ready")
        mt_done, m1_ready, m2_ready = sem("mt_done"), sem("m1_ready"), sem("m2_ready")
        m_in = sems("m_in", 2)
        st_done, exp_done, pv_done, ot_ready = sem("st_done"), sem("exp_done"), sem("pv_done"), sem("ot_ready")
        ot_t, rden_ready, ctx_ready = sem("ot_t"), sem("rden_ready"), sem("ctx_ready")

        ct_t, ctt_ready, wo_done, ao_ready, x1_ready = (sem(n) for n in ("ct_t", "ctt_ready", "wo_done", "ao_ready", "x1_ready"))
        h2_ready, h2_t, h2t_ready, lg_done, lg_ready = (sem(n) for n in ("h2_ready", "h2_t", "h2t_ready", "lg_done", "lg_ready"))
        dve_route, route_pe, exp_sc = sem("dve_route"), sem("route_pe"), sem("exp_sc")
        zero_ready, zero_out, scattered = sem("zero_ready"), sem("zero_out"), sem("scattered")
        gu_done, silu_ready, hs_ready, down_done, base_ready = (sem(n) for n in ("gu_done", "silu_ready", "hs_ready", "down_done", "base_ready"))
        xg_in = sems("xg_in", UN)
        xg_t, xgt_ready, h1_done, se_ready, he_ready, he1 = (sem(n) for n in ("xg_t", "xgt_ready", "h1_done", "se_ready", "he_ready", "he1"))
        he_t, het_ready, y_done, y_ready = (sem(n) for n in ("he_t", "het_ready", "y_done", "y_ready"))
        y_out = sems("y_out", UN)
        ga_in = sems("ga_in", 2 * NGA)
        fo1, fo_ready = sem("fo1"), sem("fo_ready")
        fo_out = sems("fo_out", NGA)

        block = stack.enter_context(nc.Block())

        def wait(eng, s, n):
            if not isinstance(n, int) or n > 0:
                eng.wait_ge(s, n)

        def over_slots(eng, step):
            for it in range(2):
                for u in range(UN):
                    step(it, u, it == 0, False)
            with eng.Fori(2, PASSES - 1) as it:
                for u in range(UN):
                    step(it, u, False, False)
            for u in range(UN):
                step(PASSES - 1, u, False, True)

        EARLY = 4 * G

        def smax_schedule(i, kt):
            s = 4 * i + 6 + kt
            return s if s < GROUPS * G else None

        OUT_AT = TB + 1
        M2_AT = 2 * TB + 2
        BE = B - 1
        COMBINED = (0, 1, 1, 2)
        AHEAD = 2

        ROUTE_DIFF = 2 * NT + 2
        ROUTE_OH = ROUTE_DIFF + 3
        ROUTE_POS = ROUTE_OH + 27
        ROUTE_EID = ROUTE_POS + 3

        @block.sync
        def _(sp):
            sp.dma_start(W["v"][:, :, :], WvT.rearrange("(c p) n -> p c n", p=P)).then_inc(w_in["v"], 16)
            sp.dma_start(W["k"][:, :, :], WkT.rearrange("(c p) n -> p c n", p=P)).then_inc(w_in["k"], 16)
            sp.dma_start(W["q"][:, :, :], WqT.rearrange("(c p) n -> p c n", p=P)).then_inc(w_in["q"], 16)
            sp.dma_start(CT[:, 1, :, :], ctxT[:, S:2 * S].rearrange("(c p) n -> p c n", p=P)).then_inc(ct_in[1], 16)
            for b in range(2, B):
                sp.dma_start(X[:, b * TB:(b + 1) * TB, :], x[b].rearrange("(t p) d -> p t d", p=P)).then_inc(x_in[b], 16)
            sp.dma_start(W["o"][:, :, :], WoT.rearrange("(c p) n -> p c n", p=P)).then_inc(w_in["o"], 16)
            def store_parts(b):
                sp.wait_ge(va_ready, TB * (b + 1))
                sp.dma_start(v_scr[b].rearrange("t p w -> p t w"), VA[:, b % 2, :, :]).then_inc(va_out[b % 2], 16)
                for j in range(4):
                    dst = k_scr if j < 2 else q_scr
                    sp.wait_ge(q1_ready, 4 * b + j + 1)
                    sp.wait_ge(q3_ready, 4 * b + j + 1)
                    sp.dma_start(dst[b, :, (j % 2) * P:(j % 2 + 1) * P, :].rearrange("a p n -> p a n"), QP[:, j, :, :])\
                      .then_inc(qp_out[j], 16)

            def parts_stored(b):
                for j in range(4):
                    sp.wait_ge(qp_out[j], 16 * (b + 1))
                sp.wait_ge(va_out[b % 2], 16 * (b // 2 + 1))

            def load_group(i):
                b, g = divmod(i, NG)
                if i >= NG:
                    sp.wait_ge(pv_done, TB * (i - NG + 1))
                rows = slice(g * G * DK, (g + 1) * G * DK)
                for t in range(TERMS):
                    sp.dma_start(QS[g][t * DK:(t + 1) * DK, :, :],
                                 q_scr[b, Q_PART[t], rows, :].rearrange("(h d) n -> d h n", h=G)).then_inc(ld_group[g], 16)
                    sp.dma_start(KST[g][t * DK:(t + 1) * DK, :, :],
                                 k_scr[b, K_PART[t], rows, :].rearrange("(h d) n -> d h n", h=G)).then_inc(ld_group[g], 16)
                sp.dma_start(VG[g][:, :, :], v_scr[b, :, :, g * G * VW:(g + 1) * G * VW].rearrange("t p w -> p t w"))\
                  .then_inc(ld_group[g], 16)

            def load_max(i):
                for part, s in ((0, m1_ready), (1, m2_ready)):
                    sp.wait_ge(s, i + 1)
                    sp.dma_start(QS[i % NG][KS + part:KS + part + 1, :, :].rearrange("p h n -> p (h n)"),
                                 mparts[:, i % 2, part, :]).then_inc(m_in[i % 2], 16)

            store_parts(0)
            parts_stored(0)
            load_group(0)
            store_parts(1)
            load_group(1)
            store_parts(2)
            load_group(2)
            store_parts(3)
            load_max(0)
            for b in range(1, B):
                parts_stored(b)
            for i in range(GROUPS):
                if i + 3 < GROUPS:
                    load_group(i + 3)
                if i + 1 < GROUPS:
                    load_max(i + 1)
                if i == 1:
                    for c in range(DC):
                        sp.dma_start(fc1[:, c, :, :], fc1_w[:, c * P:(c + 1) * P, :].rearrange("e p n -> p e n"))\
                          .then_inc(w_in["fc1"], 16)
                if i == 2:
                    for t_, src in ((wgate, gate_w), (wup, up_w), (wdown, down_w)):
                        sp.dma_start(t_[:, :, :], src.rearrange("(c p) n -> p c n", p=P)).then_inc(w_in["shared"], 16)
                    sp.dma_start(wr[:, :, :], w_router.rearrange("(c p) n -> p c n", p=P)).then_inc(w_in["router"], 16)
                if i == 3:
                    for c in range(IE // P):
                        sp.dma_start(fc2[:, c, :, :], fc2_w[:, c * P:(c + 1) * P, :].rearrange("e p n -> p e n"))\
                          .then_inc(w_in["fc2"], 16)
                if i == 4:
                    sp.wait_ge(zero_ready, 1)
                    sp.dma_start(slot_x.rearrange("(n p) d -> p n d", p=P), ZERO[:, :].unsqueeze(1).to_broadcast([P, SLOTS, D]))\
                      .then_inc(zero_out, 16)
            sp.wait_ge(scattered, 16 * 2 * NT)
            for u in range(UN):
                sp.dma_start(XG[:, u, :], slot_x[u * P:(u + 1) * P, :]).then_inc(xg_in[u], 16)

            def slot_dmas(it, u, first, last):
                j = it * UN + u
                if not last:
                    sp.wait_ge(xg_t, j + 1)
                    sp.dma_start(XG[:, u, :], slot_x[bass.ds((j + UN) * P, P), :]).then_inc(xg_in[u], 16)
                if not (first and u == 0):
                    before_u = (u - 1) % UN
                    sp.wait_ge(y_ready, j)
                    sp.dma_start(slot_y[bass.ds((j - 1) * P, P), :], YE[:, before_u, :]).then_inc(y_out[before_u], 16)

            over_slots(sp, slot_dmas)
            sp.wait_ge(y_ready, SLOTS)
            sp.dma_start(slot_y[(SLOTS - 1) * P:SLOTS * P, :], YE[:, UN - 1, :]).then_inc(y_out[UN - 1], 16)
            for t in range(NT):
                b, q = divmod(t, TB)
                sp.wait_ge(fo_ready, t + 1)
                sp.dma_start(out[b, q * P:(q + 1) * P, :], FO[:, t % NGA, :]).then_inc(fo_out[t % NGA], 16)
            for n in range(NGA):
                sp.wait_ge(fo_out[n], 16 * (NT // NGA))

        @block.gpsimd
        def _(pool):
            nc.gpsimd.memset(ident[:, :], 0.0).then_inc(const_ready, 1)
            nc.gpsimd.memset(before[:, :], 1.0).then_inc(const_ready, 1)
            nc.gpsimd.memset(ones[:, :], 1.0).then_inc(consts, 1)
            nc.gpsimd.memset(minus_half[:, :], -0.5).then_inc(consts, 1)
            nc.gpsimd.memset(ZERO[:, :], 0.0).then_inc(zero_ready, 1)
            pool.wait_ge(const_ready, 2)
            nc.gpsimd.affine_select(out=ident[:, :], in_=ident[:, :], compare_op=ALU.not_equal, fill=1.0, base=0,
                                    pattern=[[-1, P]], channel_multiplier=1).then_inc(consts, 1)
            nc.gpsimd.affine_select(out=before[:, :], in_=before[:, :], compare_op=ALU.is_gt, fill=0.0, base=0,
                                    pattern=[[1, P]], channel_multiplier=-1).then_inc(consts, 1)
            nc.gpsimd.iota(io8[:, :], [[1, E]], base=0, channel_multiplier=0,
                           allow_small_or_imprecise_dtypes=True).then_inc(consts, 1)
            nc.gpsimd.iota(io16[:, :], [[P, NT]], base=0, channel_multiplier=0,
                           allow_small_or_imprecise_dtypes=True).then_inc(consts, 1)
            nc.gpsimd.iota(io40[:, :], [[1, SLOTS]], base=0, channel_multiplier=0,
                           allow_small_or_imprecise_dtypes=True).then_inc(consts, 1)
            nc.gpsimd.memset(VA[:, :, :, :], 1.0).then_inc(va_ones, 1)
            for g in range(NG):
                pool.wait_ge(kones, g) if g else pool.wait_ge(va_ones, 1)
                nc.gpsimd.memset(KST[g][KS:KM, :, :], 1.0).then_inc(kones, 1)
            pool.wait_ge(kones, NG)
            for b in range(B):
                pool.wait_ge(ln_ve, b + 1)
                sl = slice(b * TB, (b + 1) * TB)
                nc.gpsimd.tensor_tensor(rstd[:, sl], var_eps[:, sl], minus_half[:, sl], ALU.pow).then_inc(ln_rstd, 1)
            for b in range(B):
                pool.wait_ge(ln_ve, B + b + 1)
                sl = slice(b * TB, (b + 1) * TB)
                nc.gpsimd.tensor_tensor(rstd[:, sl], var_eps[:, sl], minus_half[:, sl], ALU.pow).then_inc(ln_rstd, 1)
            pool.wait_ge(dve_route, ROUTE_POS)
            pool.wait_ge(zero_out, 16)
            for t in range(NT):
                for k in range(2):
                    nc.gpsimd.indirect_dma_start(slot_x, bass.IndirectOffsetOnAxis(ap=pos[:, k, t:t + 1], axis=0),
                                                 CH[:, t, :], None).then_inc(scattered, 16)
            for u in range(UN):
                pool.wait_ge(y_out[u], 16 * (SLOTS // UN))
            for t in range(NT):
                for k in range(2):
                    if t >= NGA:
                        pool.wait_ge(fo_ready, t - NGA + 1)
                    nc.gpsimd.indirect_dma_start(GA[:, t % NGA, k, :], None, slot_y,
                                                 bass.IndirectOffsetOnAxis(ap=pos[:, k, t:t + 1], axis=0))\
                        .then_inc(ga_in[2 * (t % NGA) + k], 16)

        @block.scalar
        def _(act):
            act.dma_start(X[:, 0:TB, :], x[0].rearrange("(t p) d -> p t d", p=P)).then_inc(x_in[0], 16)
            act.dma_start(CT[:, 0, :, :], ctxT[:, 0:S].rearrange("(c p) n -> p c n", p=P)).then_inc(ct_in[0], 16)
            act.dma_start(X[:, TB:2 * TB, :], x[1].rearrange("(t p) d -> p t d", p=P)).then_inc(x_in[1], 16)
            for n, (t_, src) in enumerate(((bias_qk[:, 0, :], bq), (bias_qk[:, 1, :], bk))):
                act.dma_start(t_, src).then_inc(w_in["small"], 16)
            for t_, src in ((bv_row, bv), (bo_row, bo)):
                act.dma_start(t_[:, :], src.partition_broadcast(P)).then_inc(w_in["small"], 16)
            for n, src in enumerate((g_xattn, g_ffn)):
                act.dma_start(gates[:, n:n + 1], src.partition_broadcast(P)).then_inc(w_in["small"], 16)
            act.wait_ge(w_in["small"], 96)
            nc.scalar.activation(tg[:, :], gates[:, :], ACT.Tanh).then_inc(scaled, 1)
            nc.scalar.activation(bias_sc[:, 0, :], bias_qk[:, 0, :], ACT.Copy, scale=0.25).then_inc(scaled, 1)
            nc.scalar.activation(bias_sc[:, 1, :], bias_qk[:, 1, :], ACT.Copy).then_inc(scaled, 1)
            act.wait_ge(scaled, 3)
            def xnt_first(b):
                act.wait_ge(xt_done, 2 * b + 1)
                if b >= 2:
                    act.wait_ge(qk_done, 4 * (b - 1))
                nc.scalar.copy(XNT[:, b % 2, 0, :], PS[:, 0, :]).then_inc(xnt_ready, 1)

            xnt_first(0)
            for b in range(B):
                for j in range(4):
                    if j == 2 and b + 1 < B:
                        xnt_first(b + 1)
                    act.wait_ge(qk_done, 4 * b + j + 1)
                    if j == 1 and b + 2 < B:
                        act.wait_ge(v_done, 2 * (b + 1))
                        act.dma_start(CT[:, b % 2, :, :], ctxT[:, (b + 2) * S:(b + 3) * S]
                                      .rearrange("(c p) n -> p c n", p=P)).then_inc(ct_in[b % 2], 16)
                    if b:
                        act.wait_ge(qr_ready, 4 * (b - 1) + j + 1)
                    bias = bias_sc[:, 1 - j // 2, j % 2:j % 2 + 1]
                    scale = 1.0 if j < 2 else 0.25
                    nc.scalar.activation(QF[:, j, :], PS[:, 2 + j % 2, :], ACT.Identity, bias=bias, scale=scale).then_inc(qf_ready, 1)
                    if b:
                        act.wait_ge(qp_out[j], 16 * b)
                    nc.scalar.activation(QP[:, j, 0, :], PS[:, 2 + j % 2, :], ACT.Identity, bias=bias, scale=scale).then_inc(q1_ready, 1)
            def m_first(i):
                act.wait_ge(mt_done, i + 1)
                if i >= 2:
                    act.wait_ge(m_in[i % 2], 32 * (i // 2))
                nc.scalar.copy(mparts[:, i % 2, 0, :], PS[0:G * TB, 7, 0:P]).then_inc(m1_ready, 1)

            def out_copy(i):
                act.wait_ge(pv_done, TB * (i + 1))
                if i >= 2:
                    act.wait_ge(ot_t, i - 1)
                nc.scalar.copy(OT[i % 2], PS[:, 6, :]).then_inc(ot_ready, 1)

            for i in range(GROUPS):
                if i == 0:
                    m_first(0)
                for kt in range(TB):
                    for j in range(G):
                        act.wait_ge(st_done, G * (TB * i + kt) + j + 1)
                        if i:
                            act.wait_ge(pv_done, TB * (i - 1) + kt + 1)
                        nc.scalar.activation(PT[:, kt, j, :], PS[:, j, :], ACT.Exp).then_inc(exp_done, 1)
                        if j == 2 and kt == 0 and i:
                            out_copy(i - 1)
                        if j == 2 and kt == 2 and i + 1 < GROUPS:
                            m_first(i + 1)
            out_copy(GROUPS - 1)
            def ctt_first(b):
                act.wait_ge(ct_t, 2 * b + 1)
                if b >= 2:
                    act.wait_ge(wo_done, 2 * (b - 1))
                nc.scalar.copy(CTT[:, b % 2, 0, :], PS[:, 0, :]).then_inc(ctt_ready, 1)

            def h2t_first(b):
                act.wait_ge(h2_t, 2 * b + 1)
                nc.scalar.copy(H2T[:, 0, b * S:(b + 1) * S], PS[:, 4, :]).then_inc(h2t_ready, 1)

            def silu(b, c):
                n = IC * b + c
                act.wait_ge(gu_done, n + 1)
                if n >= 2:
                    act.wait_ge(hs_ready, n - 1)
                nc.scalar.activation(SG[:, n % 2, :], PS[:, 2 * (n % 2), :], ACT.Silu).then_inc(silu_ready, 1)

            for b in range(B):
                ctt_first(b)
                if b:
                    h2t_first(b - 1)
            for c in range(AHEAD):
                silu(0, c)
            h2t_first(B - 1)
            for c in range(AHEAD, IC):
                silu(0, c)
            for b in range(1, BE):
                for c in range(IC):
                    silu(b, c)
            act.wait_ge(dve_route, ROUTE_DIFF)
            nc.scalar.activation(sc[:, 1, :], sc[:, 0, :], ACT.Exp).then_inc(exp_sc, 1)
            act.wait_ge(xg_t, 1)
            nc.scalar.copy(XGT[:, 0, :], PS[:, 0, 0:D]).then_inc(xgt_ready, 1)

            def slot_acts(it, u, first, last):
                j = it * UN + u
                act.wait_ge(h1_done, j + 1)
                if not first:
                    act.wait_ge(he_ready, j - UN + 1)
                nc.scalar.activation(SE[:, u, :], PS[:, 1 + u, 0:IE], ACT.Silu).then_inc(se_ready, 1)
                if not (last and u == UN - 1):
                    act.wait_ge(xg_t, j + 2)
                    nc.scalar.copy(XGT[:, (u + 1) % UN, :], PS[:, 0, 0:D]).then_inc(xgt_ready, 1)
                act.wait_ge(he_t, j + 1)
                nc.scalar.copy(HET[:, u, :], PS[:, 4, 0:IE]).then_inc(het_ready, 1)

            over_slots(act, slot_acts)
            for b in range(BE, B):
                for c in range(IC):
                    silu(b, c)

        @block.vector
        def _(dve):

            def layernorm(b, n0):
                sl = slice(b * TB, (b + 1) * TB)
                for t in range(TB):
                    nc.vector.bn_stats(stats[:, b * TB + t, :], X[:, b * TB + t, :]).then_inc(ln_stats, 1)
                dve.wait_ge(ln_stats, 4 * (n0 + b + 1))
                for t in range(TB):
                    nc.vector.bn_aggr(mv[:, b * TB + t, :], stats[:, b * TB + t, :]).then_inc(ln_mv, 1)
                dve.wait_ge(ln_mv, 4 * (n0 + b + 1))
                nc.vector.tensor_scalar(var_eps[:, sl], mv[:, sl, 1], EPS, None, ALU.add).then_inc(ln_ve, 1)

            def normalise(b, n0, dst, ready):
                dve.wait_ge(ln_rstd, n0 + b + 1)
                for t in range(TB):
                    tt = b * TB + t
                    nc.vector.tensor_scalar(dst(t), X[:, tt, :], mv[:, tt, 0:1], rstd[:, tt:tt + 1],
                                            ALU.subtract, ALU.mult).then_inc(ready, 1)

            def one_max(n):
                s, qt = divmod(n, TB)
                i, j = divmod(s, G)
                dve.wait_ge(smax_done, n + 1)
                if n % 16 == 0 and i >= 2:
                    dve.wait_ge(mt_done, i - 1)
                nc.vector.tensor_reduce(nmax[:, i % 2, j * TB + qt:j * TB + qt + 1], PS[:, 4 + n % 2, :], AX.X,
                                        ALU.max, negate=True).then_inc(max_ready, 1)

            early = iter(range(EARLY))

            def early_max(b):
                if b >= 2:
                    n = next(early, None)
                    if n is not None:
                        one_max(n)

            for b in range(2):
                dve.wait_ge(x_in[b], 16)
                layernorm(b, 0)
            normalise(0, 0, lambda t: XN[:, 0, t, :], xn_ready)
            dve.wait_ge(w_in["small"], 96)
            dve.wait_ge(va_ones, 1)
            dve.wait_ge(xt_done, 2)
            nc.vector.tensor_copy(XNT[:, 0, 1, :], PS[:, 1, :]).then_inc(xnt_ready, 1)
            for b in range(B):
                s = b % 2
                if b + 1 < B:
                    if b:
                        dve.wait_ge(xt_done, 2 * b)
                    normalise(b + 1, 0, lambda t: XN[:, (b + 1) % 2, t, :], xn_ready)
                if b >= 2:
                    dve.wait_ge(va_out[s], 16 * (b // 2))
                for t in range(TB):
                    dve.wait_ge(v_done, 2 * b + t // 2 + 1)
                    nc.vector.tensor_tensor(
                        VA[:, s, t, :].rearrange("p (h w) -> p h w", w=VW)[:, :, 0:DK],
                        PS[:, 6 + t // 2, (t % 2) * D:(t % 2 + 1) * D].rearrange("p (h w) -> p h w", w=DK),
                        bv_row[:, :].rearrange("p (h w) -> p h w", w=DK), ALU.add).then_inc(va_ready, 1)
                    early_max(b)
                for j in range(4):
                    n = 4 * b + j
                    dve.wait_ge(qf_ready, n + 1)
                    dve.wait_ge(q1_ready, n + 1)
                    if n >= 2:
                        dve.wait_ge(q3_ready, n - 1)
                    nc.vector.tensor_tensor(RQ[:, n % 2, :], QF[:, j, :], QP[:, j, 0, :], ALU.subtract).then_inc(qr_ready, 1)
                    dve.wait_ge(qr_ready, n + 1)
                    if b:
                        dve.wait_ge(qp_out[j], 16 * b)
                    nc.vector.tensor_copy(QP[:, j, 1, :], RQ[:, n % 2, :]).then_inc(q2_ready, 1)
                    early_max(b)
                    dve.wait_ge(q2_ready, n + 1)
                    nc.vector.tensor_tensor(QP[:, j, 2, :], RQ[:, n % 2, :], QP[:, j, 1, :], ALU.subtract).then_inc(q3_ready, 1)
                    if j == 1 and b + 1 < B:
                        dve.wait_ge(xt_done, 2 * b + 4)
                        if b >= 1:
                            dve.wait_ge(qk_done, 4 * b)
                        nc.vector.tensor_copy(XNT[:, (b + 1) % 2, 1, :], PS[:, 1, :]).then_inc(xnt_ready, 1)
                if b + 2 < B:
                    dve.wait_ge(x_in[b + 2], 16)
                    layernorm(b + 2, 0)

            def head_max(s):
                for qt in range(TB):
                    one_max(TB * s + qt)

            def m_second(i):
                dve.wait_ge(m1_ready, i + 1)
                nc.vector.tensor_tensor(mparts[:, i % 2, 1, :], PS[0:G * TB, 7, 0:P], mparts[:, i % 2, 0, :],
                                        ALU.subtract).then_inc(m2_ready, 1)

            def denominators(i):
                dve.wait_ge(ot_t, i + 1)
                if i >= 2:
                    dve.wait_ge(ctx_ready, TB * (i - 1))
                o = PS[:, 7, :].rearrange("p (q h w) -> p q h w", q=TB, h=G)
                nc.vector.reciprocal(rden[:, i % 2, :, :], o[:, :, :, DK]).then_inc(rden_ready, 1)

            def head_out(i, qt):
                b, g = divmod(i, NG)
                dve.wait_ge(rden_ready, i + 1)
                o = PS[:, 7, qt * P:(qt + 1) * P].rearrange("p (h w) -> p h w", h=G)
                nc.vector.tensor_tensor(
                    CH[:, b * TB + qt, g * G * DK:(g + 1) * G * DK].rearrange("p (h w) -> p h w", h=G),
                    o[:, :, 0:DK], rden[:, i % 2, qt, :].unsqueeze(2).to_broadcast([P, G, DK]),
                    ALU.mult).then_inc(ctx_ready, 1)

            m_second(0)
            for n in early:
                one_max(n)
            for n in range(EARLY, 6 * TB):
                one_max(n)
            for i in range(GROUPS):
                for kt in range(TB):
                    s = smax_schedule(i, kt)
                    for qt in range(TB):
                        if s is not None:
                            one_max(TB * s + qt)
                        if i:
                            n = TB * kt + qt - OUT_AT
                            if n == 0:
                                denominators(i - 1)
                            elif 0 < n <= TB:
                                head_out(i - 1, n - 1)
                        if TB * kt + qt == M2_AT and i + 1 < GROUPS:
                            m_second(i + 1)
            denominators(GROUPS - 1)
            for qt in range(TB):
                head_out(GROUPS - 1, qt)

            dve.wait_ge(w_in["small"], 96)
            dve.wait_ge(scaled, 3)

            def ctt_second(b):
                dve.wait_ge(ct_t, 2 * b + 2)
                if b >= 2:
                    dve.wait_ge(wo_done, 2 * (b - 1))
                nc.vector.tensor_copy(CTT[:, b % 2, 1, :], PS[:, 1, :]).then_inc(ctt_ready, 1)

            def residual(b):
                for h in range(2):
                    n = 2 * b + h
                    dve.wait_ge(wo_done, n + 1)
                    if n >= 4:
                        dve.wait_ge(x1_ready, n - 3)
                    tt = slice(b * TB + 2 * h, b * TB + 2 * h + 2)
                    nc.vector.tensor_tensor(AO[:, n % 4, :].rearrange("p (t d) -> p t d", t=2),
                                            PS[:, 2 + h, :].rearrange("p (t d) -> p t d", t=2),
                                            bo_row[:, :].unsqueeze(1).to_broadcast([P, 2, D]), ALU.add).then_inc(ao_ready, 1)
                    dve.wait_ge(ao_ready, n + 1)
                    nc.vector.scalar_tensor_tensor(out=X[:, tt, :], in0=AO[:, n % 4, :].rearrange("p (t d) -> p t d", t=2),
                                                   scalar=tg[:, 0:1], in1=X[:, tt, :], op0=ALU.mult, op1=ALU.add)\
                        .then_inc(x1_ready, 1)
                dve.wait_ge(x1_ready, 2 * b + 2)
                layernorm(b, B)

            def h2t_second(b):
                dve.wait_ge(h2_t, 2 * b + 2)
                nc.vector.tensor_copy(H2T[:, 1, b * S:(b + 1) * S], PS[:, 5, :]).then_inc(h2t_ready, 1)

            def logits(b):
                dve.wait_ge(lg_done, b + 1)
                nc.vector.tensor_copy(LG[:, b * TB:(b + 1) * TB, :],
                                      PS[:, 6, 0:TB * E].rearrange("p (t e) -> p t e", t=TB)).then_inc(lg_ready, 1)

            def hidden(b, c):
                n = IC * b + c
                dve.wait_ge(silu_ready, n + 1)
                if b >= 2:
                    dve.wait_ge(down_done, 2 * (b - 1))
                nc.vector.tensor_tensor(HS[:, b % 2, c, :], SG[:, n % 2, :], PS[:, 2 * (n % 2) + 1, :], ALU.mult)\
                    .then_inc(hs_ready, 1)

            def shared_out(b, h):
                dve.wait_ge(down_done, 2 * b + h + 1)
                tt = slice(b * TB + 2 * h, b * TB + 2 * h + 2)
                nc.vector.scalar_tensor_tensor(out=X[:, tt, :], in0=PS[:, 6 + h, :].rearrange("p (t d) -> p t d", t=2),
                                               scalar=tg[:, 1:2], in1=X[:, tt, :], op0=ALU.mult, op1=ALU.add)\
                    .then_inc(base_ready, 1)

            for b in range(B):
                ctt_second(b)
                if b:
                    normalise(b - 1, B, lambda t: CH[:, (b - 1) * TB + t, :], h2_ready)
                residual(b)
                if b:
                    h2t_second(b - 1)
                    if b < B - 1:
                        logits(b - 1)
            normalise(B - 1, B, lambda t: CH[:, (B - 1) * TB + t, :], h2_ready)
            logits(B - 2)
            for c in range(AHEAD):
                hidden(0, c)
            h2t_second(B - 1)
            logits(B - 1)

            chain = [0]

            def step(ins):
                chain[0] += 1
                ins.then_inc(dve_route, 1)
                dve.wait_ge(dve_route, chain[0])

            def many(instructions):
                for ins in instructions:
                    chain[0] += 1
                    ins.then_inc(dve_route, 1)
                dve.wait_ge(dve_route, chain[0])

            dve.wait_ge(lg_ready, B)
            dve.wait_ge(consts, 7)
            many(nc.vector.max(mx8[:, t, :], LG[:, t, :]) for t in range(NT))
            many(nc.vector.max_index(ix8[:, t, :], mx8[:, t, :], LG[:, t, :]) for t in range(NT))
            step(nc.vector.tensor_copy(ixf[:, :, :], ix8[:, :, 0:2]))
            step(nc.vector.tensor_tensor(sc[:, 0, :], mx8[:, :, 1], mx8[:, :, 0], ALU.subtract))
            assert chain[0] == ROUTE_DIFF
            for k in range(2):
                step(nc.vector.tensor_tensor(OH[:, k, :, :], io8[:, :].unsqueeze(1).to_broadcast([P, NT, E]),
                                             ixf[:, :, k].unsqueeze(2).to_broadcast([P, NT, E]), ALU.is_equal))
            step(nc.vector.tensor_tensor(OH[:, 2, :, :], OH[:, 0, :, :], OH[:, 1, :, :], ALU.add))
            assert chain[0] == ROUTE_OH
            hidden(0, AHEAD)
            dve.wait_ge(route_pe, 2)
            tot = PS[:, 5, 0:NT * E].rearrange("p (t e) -> p t e", t=NT)
            rank = PS[:, 4, 0:NT * E].rearrange("p (t e) -> p t e", t=NT)
            step(nc.vector.tensor_copy(CU[:, 0, :, :], tot))
            a = 0
            for d in (1, 2, 4, 8):
                many([nc.vector.tensor_copy(CU[:, 1 - a, 0:d, :], CU[:, a, 0:d, :]),
                      nc.vector.tensor_tensor(CU[:, 1 - a, d:NT, :], CU[:, a, d:NT, :], CU[:, a, 0:NT - d, :], ALU.add)])
                a = 1 - a
            step(nc.vector.tensor_tensor(cnt_gt[:, :, :], CU[:, a, NT - 1, :].unsqueeze(2).to_broadcast([P, E, NT]),
                                         io16[:, :].unsqueeze(1).to_broadcast([P, E, NT]), ALU.is_gt))
            step(nc.vector.tensor_reduce(tl[:, 0, :], cnt_gt[:, :, :], AX.X, ALU.add))
            src = 0
            for n, d in enumerate((1, 2, 4)):
                to = n + 1
                many([nc.vector.tensor_copy(tl[:, to, 0:d], tl[:, src, 0:d]),
                      nc.vector.tensor_tensor(tl[:, to, d:E], tl[:, src, d:E], tl[:, src, 0:E - d], ALU.add)])
                src = to
            step(nc.vector.tensor_tensor(pos_base[:, :, :], CU[:, a, :, :], rank, ALU.add))
            step(nc.vector.tensor_tensor(CU[:, 1 - a, :, :], pos_base[:, :, :], tot, ALU.subtract))
            step(nc.vector.tensor_tensor(tl[:, 1, :], tl[:, 3, :], tl[:, 0, :], ALU.subtract))
            step(nc.vector.tensor_scalar(tl[:, 2, :], tl[:, 1, :], float(P), None, ALU.mult))
            step(nc.vector.tensor_tensor(pos_base[:, :, :], CU[:, 1 - a, :, :],
                                         tl[:, 2, :].unsqueeze(1).to_broadcast([P, NT, E]), ALU.add))
            for k in range(2):
                step(nc.vector.tensor_tensor(CU[:, k, :, :], OH[:, k, :, :], pos_base[:, :, :], ALU.mult))
                step(nc.vector.tensor_reduce(posf[:, k, :], CU[:, k, :, :], AX.X, ALU.add))
            step(nc.vector.tensor_copy(pos[:, :, :], posf[:, :, :]))
            assert chain[0] == ROUTE_POS, chain[0]
            step(nc.vector.tensor_tensor(ge[:, :, :], io40[:, :].unsqueeze(2).to_broadcast([P, SLOTS, E]),
                                         tl[:, 3, :].unsqueeze(1).to_broadcast([P, SLOTS, E]), ALU.is_ge))
            step(nc.vector.tensor_reduce(eidf[:, :], ge[:, :, :], AX.X, ALU.add))
            step(nc.vector.tensor_scalar(eid[:, :], eidf[0:1, :], float(E - 1), None, ALU.min))
            assert chain[0] == ROUTE_EID, chain[0]
            for c in range(AHEAD + 1, IC):
                hidden(0, c)
            for h in range(2):
                shared_out(0, h)
            for b in range(1, BE):
                for c in range(IC):
                    hidden(b, c)
                for h in range(2):
                    shared_out(b, h)
            dve.wait_ge(exp_sc, 1)
            step(nc.vector.tensor_scalar(sc[:, 2, :], sc[:, 1, :], 1.0, None, ALU.add))
            step(nc.vector.reciprocal(sc[:, 3, :], sc[:, 2, :]))
            step(nc.vector.tensor_tensor(sc[:, 0, :], sc[:, 1, :], sc[:, 3, :], ALU.mult))
            step(nc.vector.tensor_scalar(scg[:, 0, :], sc[:, 3, :], tg[:, 1:2], None, ALU.mult))
            step(nc.vector.tensor_scalar(scg[:, 1, :], sc[:, 0, :], tg[:, 1:2], None, ALU.mult))

            def slot_result(it, u, first):
                dve.wait_ge(y_done, it * UN + u + 1)
                if not first:
                    dve.wait_ge(y_out[u], it * 16)
                nc.vector.tensor_copy(YE[:, u, :], PS[:, 5 + u, 0:D]).then_inc(y_ready, 1)

            def slot_products(it, u, first, last):
                dve.wait_ge(se_ready, it * UN + u + 1)
                if not first:
                    dve.wait_ge(he_t, (it - 1) * UN + u + 1)
                nc.vector.tensor_tensor(HE[:, u, :], SE[:, u, :], PS[:, 1 + u, IE:I2], ALU.mult).then_inc(he_ready, 1)
                if u:
                    slot_result(it, u - 1, first)
                elif not first:
                    slot_result(it - 1, UN - 1, isinstance(it, int) and it == 1)

            over_slots(dve, slot_products)
            slot_result(PASSES - 1, UN - 1, False)
            def combine(t):
                n = t % NGA
                dve.wait_ge(ga_in[2 * n], 16 * (t // NGA + 1))
                dve.wait_ge(ga_in[2 * n + 1], 16 * (t // NGA + 1))
                dve.wait_ge(base_ready, 2 * (t // TB + 1))
                nc.vector.scalar_tensor_tensor(out=X[:, t, :], in0=GA[:, n, 0, :], scalar=scg[:, 0, t:t + 1],
                                               in1=X[:, t, :], op0=ALU.mult, op1=ALU.add).then_inc(fo1, 1)
                dve.wait_ge(fo1, t + 1)
                if t >= NGA:
                    dve.wait_ge(fo_out[n], 16 * (t // NGA))
                nc.vector.scalar_tensor_tensor(out=FO[:, n, :], in0=GA[:, n, 1, :], scalar=scg[:, 1, t:t + 1],
                                               in1=X[:, t, :], op0=ALU.mult, op1=ALU.add).then_inc(fo_ready, 1)

            done = iter(range(NT))
            for c, tiles in zip(range(IC), COMBINED):
                hidden(B - 1, c)
                for _ in range(tiles):
                    combine(next(done))
            for h in range(2):
                shared_out(B - 1, h)
                combine(next(done))
            for t in done:
                combine(t)

        @block.tensor
        def _(pe):
            mm = nc.tensor.matmul
            pe.wait_ge(consts, 3)
            def rows_transpose(b):
                for c in range(DC):
                    pe.wait_ge(xn_ready, TB * (b + 1))
                    if b:
                        pe.wait_ge(xnt_ready, 2 * b)
                    for t in range(TB):
                        last = nc.tensor.transpose(PS[:, c, t * P:(t + 1) * P], XN[:, b % 2, t, c * P:(c + 1) * P], ident[:, :])
                    last.then_inc(xt_done, 1)

            def scores_for_max(n):
                s, qt = divmod(n, TB)
                i, j = divmod(s, G)
                b, g = divmod(i, NG)
                if j == 0 and qt == 0:
                    pe.wait_ge(ld_group[g], 16 * (2 * TERMS + 1) * (b + 1))
                if n >= 2:
                    pe.wait_ge(max_ready, n - 1)
                mm(PS[:, 4 + n % 2, :], QS[g][0:KS, j, qt * P:(qt + 1) * P], KST[g][0:KS, j, :],
                   start=True, stop=True).then_inc(smax_done, 1)

            early = iter(range(EARLY))

            def early_scores(b):
                if b >= 2:
                    n = next(early, None)
                    if n is not None:
                        scores_for_max(n)

            rows_transpose(0)
            for b in range(B):
                s = b % 2
                pe.wait_ge(w_in["v"], 16)
                pe.wait_ge(ct_in[s], 16 * (b // 2 + 1))
                for t in range(TB):
                    if b:
                        pe.wait_ge(va_ready, TB * b)
                    for c in range(DC):
                        last = mm(PS[:, 6 + t // 2, (t % 2) * D:(t % 2 + 1) * D], CT[:, s, c, t * P:(t + 1) * P],
                                  W["v"][:, c, :], start=(c == 0), stop=(c == DC - 1))
                    if t % 2:
                        last.then_inc(v_done, 1)
                    early_scores(b)
                for j in range(4):
                    n = 4 * b + j
                    if j == 2:
                        if b + 1 < B:
                            rows_transpose(b + 1)
                        pe.wait_ge(xnt_ready, 2 * (b + 1))
                    if n >= 2:
                        pe.wait_ge(q1_ready, n - 1)
                    pe.wait_ge(w_in["k" if j < 2 else "q"], 16)
                    w, src = (W["k"], CT) if j < 2 else (W["q"], XNT)
                    for c in range(DC):
                        last = mm(PS[:, 2 + j % 2, :], w[:, c, (j % 2) * P:(j % 2 + 1) * P], src[:, s, c, :],
                                  start=(c == 0), stop=(c == DC - 1))
                    last.then_inc(qk_done, 1)
                    early_scores(b)

            def max_transpose(i):
                pe.wait_ge(max_ready, TB * G * (i + 1))
                if i == 0:
                    pe.wait_ge(va_ready, TB * B)
                if i >= 2:
                    pe.wait_ge(ctx_ready, TB * (i - 1))
                nc.tensor.transpose(PS[0:G * TB, 7, 0:P], nmax[:, i % 2, :], ident[:, :]).then_inc(mt_done, 1)

            def values(i, kt):
                g = i % NG
                pe.wait_ge(exp_done, G * (TB * i + kt + 1))
                if kt == 0 and i:
                    pe.wait_ge(ot_ready, i)
                if kt == 0 and i == 0:
                    pe.wait_ge(va_ready, TB * B)
                for j in range(G):
                    last = mm(PS[32 * j:32 * j + VW, 6, :], VG[g][:, kt, j * VW:(j + 1) * VW], PT[:, kt, j, :],
                              start=(kt == 0), stop=(kt == TB - 1), tile_position=(0, 32 * j))
                last.then_inc(pv_done, 1)

            def out_transpose(i):
                pe.wait_ge(ot_ready, i + 1)
                pe.wait_ge(m2_ready, min(i + 2, GROUPS))
                wait(pe, ctx_ready, TB * i)
                for qt in range(TB):
                    last = nc.tensor.transpose(PS[:, 7, qt * P:(qt + 1) * P], OT[i % 2][:, qt * P:(qt + 1) * P], ident[:, :])
                last.then_inc(ot_t, 1)

            max_transpose(0)
            for n in early:
                scores_for_max(n)
            for n in range(EARLY, 6 * TB):
                scores_for_max(n)
            pe.wait_ge(q1_ready, 4 * B)
            for i in range(GROUPS):
                b, g = divmod(i, NG)
                pe.wait_ge(m_in[i % 2], 32 * (i // 2 + 1))
                if i < NG:
                    pe.wait_ge(kones, g + 1)

                def scores(kt, j):
                    n = G * (TB * i + kt) + j
                    if n >= G:
                        pe.wait_ge(exp_done, n - G + 1)
                    mm(PS[:, j, :], KST[g][0:KM, j, kt * P:(kt + 1) * P], QS[g][0:KM, j, :],
                       start=True, stop=True).then_inc(st_done, 1)

                for kt in range(TB):
                    s = smax_schedule(i, kt)
                    mx = [lambda n=TB * s + qt: scores_for_max(n) for qt in range(TB)] if s is not None else \
                        [lambda: None] * TB
                    scores(kt, 0)
                    scores(kt, 1)
                    mx[0]()
                    scores(kt, 2)
                    mx[1]()
                    if kt:
                        values(i, kt - 1)
                    elif i:
                        values(i - 1, TB - 1)
                    if kt == 1 and i:
                        out_transpose(i - 1)
                    mx[2]()
                    if kt == 2 and i + 1 < GROUPS:
                        max_transpose(i + 1)
                    scores(kt, 3)
                    mx[3]()
            values(GROUPS - 1, TB - 1)
            out_transpose(GROUPS - 1)

            def ctx_transpose(b):
                for c in range(DC):
                    pe.wait_ge(ctx_ready, TB * NG * (b + 1))
                    if b == 0:
                        pe.wait_ge(exp_done, G * TB * GROUPS)
                    else:
                        pe.wait_ge(ctt_ready, 2 * b)
                    for t in range(TB):
                        last = nc.tensor.transpose(PS[:, c, t * P:(t + 1) * P], CH[:, b * TB + t, c * P:(c + 1) * P], ident[:, :])
                    last.then_inc(ct_t, 1)

            def out_projection(b):
                pe.wait_ge(w_in["o"], 16)
                pe.wait_ge(ctt_ready, 2 * (b + 1))
                for t in range(TB):
                    if b:
                        pe.wait_ge(ao_ready, 2 * (b - 1) + t // 2 + 1)
                    for c in range(DC):
                        last = mm(PS[:, 2 + t // 2, (t % 2) * D:(t % 2 + 1) * D], CTT[:, b % 2, c, t * P:(t + 1) * P],
                                  W["o"][:, c, :], start=(c == 0), stop=(c == DC - 1))
                    if t % 2:
                        last.then_inc(wo_done, 1)

            def router(b):
                for c in range(DC):
                    pe.wait_ge(h2_ready, TB * (b + 1))
                    if b:
                        pe.wait_ge(h2t_ready, 2 * b)
                    for t in range(TB):
                        last = nc.tensor.transpose(PS[:, 4 + c, t * P:(t + 1) * P], CH[:, b * TB + t, c * P:(c + 1) * P], ident[:, :])
                    last.then_inc(h2_t, 1)
                pe.wait_ge(w_in["router"], 16)
                pe.wait_ge(h2t_ready, 2 * (b + 1))
                if b:
                    pe.wait_ge(lg_ready, b)
                for t in range(TB):
                    for c in range(DC):
                        last = mm(PS[:, 6, t * E:(t + 1) * E], H2T[:, c, b * S + t * P:b * S + (t + 1) * P], wr[:, c, :],
                                  start=(c == 0), stop=(c == DC - 1))
                last.then_inc(lg_done, 1)

            def gate_up(b, c):
                n = IC * b + c
                if n == 0:
                    pe.wait_ge(w_in["shared"], 48)
                    pe.wait_ge(ctt_ready, 2 * B)
                    pe.wait_ge(ao_ready, 2 * B)
                if n >= 2:
                    pe.wait_ge(hs_ready, n - 1)
                for k, w in enumerate((wgate, wup)):
                    for d in range(DC):
                        last = mm(PS[:, 2 * (n % 2) + k, :], w[:, d, c * P:(c + 1) * P], H2T[:, d, b * S:(b + 1) * S],
                                  start=(d == 0), stop=(d == DC - 1))
                last.then_inc(gu_done, 1)

            def down(b):
                pe.wait_ge(hs_ready, IC * (b + 1))
                pe.wait_ge(lg_ready, B)
                for t in range(TB):
                    if b:
                        pe.wait_ge(base_ready, 2 * (b - 1) + t // 2 + 1)
                    for c in range(IC):
                        last = mm(PS[:, 6 + t // 2, (t % 2) * D:(t % 2 + 1) * D], HS[:, b % 2, c, t * P:(t + 1) * P],
                                  wdown[:, c, :], start=(c == 0), stop=(c == IC - 1))
                    if t % 2:
                        last.then_inc(down_done, 1)

            for b in range(B):
                ctx_transpose(b)
                out_projection(b)
                if b:
                    router(b - 1)
            for c in range(AHEAD):
                gate_up(0, c)
            router(B - 1)
            for c in range(AHEAD, IC):
                gate_up(0, c)
                if c == AHEAD:
                    pe.wait_ge(dve_route, ROUTE_OH)
                    pe.wait_ge(consts, 7)
                    choice = OH[:, 2, :, :].rearrange("p t e -> p (t e)")
                    mm(PS[:, 4, 0:NT * E], before[:, :], choice, start=True, stop=True).then_inc(route_pe, 1)
                    mm(PS[:, 5, 0:NT * E], ones[:, :], choice, start=True, stop=True).then_inc(route_pe, 1)
            down(0)
            for b in range(1, BE):
                for c in range(IC):
                    gate_up(b, c)
                down(b)

            pe.wait_ge(w_in["fc1"], 32)
            pe.wait_ge(w_in["fc2"], 32)
            pe.wait_ge(dve_route, ROUTE_EID)
            pe.wait_ge(base_ready, 2 * BE)
            expert = [pe.alloc_register(f"expert{u}") for u in range(UN)]

            def expert_of(u):
                return bass.ds(pe.snap(expert[u], min_val=0, max_val=E - 1), 1)

            def transpose_rows(it, u, first):
                pe.wait_ge(xg_in[u], (it + 1) * 16)
                if not (first and u == 0):
                    pe.wait_ge(xgt_ready, it * UN + u)
                for c in range(DC):
                    last = nc.tensor.transpose(PS[:, 0, c * P:(c + 1) * P], XG[:, u, c * P:(c + 1) * P], ident[:, :])
                last.then_inc(xg_t, 1)

            def second_product(it, u, first):
                e = expert_of(u)
                pe.wait_ge(het_ready, it * UN + u + 1)
                if not first:
                    pe.wait_ge(y_ready, (it - 1) * UN + u + 1)
                for c in range(IE // P):
                    last = mm(PS[:, 5 + u, 0:D], HET[:, u, c * P:(c + 1) * P], fc2[:, c, e, :],
                              start=(c == 0), stop=(c == IE // P - 1))
                last.then_inc(y_done, 1)

            def slot_matmuls(it, u, first, last):
                j = it * UN + u
                e = expert_of(u)
                pe.wait_ge(xgt_ready, j + 1)
                if not first:
                    pe.wait_ge(he_ready, (it - 1) * UN + u + 1)
                for c in range(DC):
                    last_mm = mm(PS[:, 1 + u, :], XGT[:, u, c * P:(c + 1) * P], fc1[:, c, e, :],
                                 start=(c == 0), stop=(c == DC - 1))
                last_mm.then_inc(h1_done, 1)
                if not (last and u == UN - 1):
                    pe.reg_load(expert[(u + 1) % UN], eid[0:1, bass.ds(j + 1, 1)])
                if u < UN - 1:
                    transpose_rows(it, u + 1, first)
                elif not last:
                    transpose_rows(it + 1, 0, False)
                if u:
                    second_product(it, u - 1, first)
                elif not first:
                    second_product(it - 1, UN - 1, isinstance(it, int) and it == 1)
                pe.wait_ge(he_ready, j + 1)
                if not (first and u == 0):
                    pe.wait_ge(het_ready, j)
                for c in range(IE // P):
                    last_mm = nc.tensor.transpose(PS[:, 4, c * P:(c + 1) * P], HE[:, u, c * P:(c + 1) * P], ident[:, :])
                last_mm.then_inc(he_t, 1)

            pe.reg_load(expert[0], eid[0:1, 0:1])
            transpose_rows(0, 0, True)
            over_slots(pe, slot_matmuls)
            second_product(PASSES - 1, UN - 1, False)
            pe.wait_ge(xgt_ready, SLOTS)
            pe.wait_ge(he_ready, SLOTS)
            for b in range(BE, B):
                for c in range(IC):
                    gate_up(b, c)
                pe.wait_ge(y_ready, SLOTS)
                down(b)


_INS = ['x', 'ctx_1024T', 'g_xattn', 'g_ffn', 'WqT', 'bq', 'WkT', 'bk', 'WvT', 'bv', 'WoT', 'bo',
        'w_router', 'fc1_w', 'fc2_w', 'gate_w', 'up_w', 'down_w']


def kernel(**inputs):
    import numpy as _np
    import concourse.bacc as _bacc
    from concourse.bass_utils import run_bass_kernel_spmd as _run

    a = {k: _np.asarray(v) for k, v in inputs.items()}
    B, S, D = a['x'].shape
    laid = [
        a['x'],
        a['ctx_1024'].reshape(B * S, D).T,
        a['g_xattn'], a['g_ffn'],
    ]
    for n in 'qkvo':
        b = a[f'L0_xattn_b{n}']
        laid += [a[f'L0_xattn_W{n}'].T, b.reshape(-1, P).T if n in 'qk' else b]
    laid += [a[f'L0_ffn_{n}'] for n in ('w_router', 'fc1_w', 'fc2_w', 'gate_w', 'up_w', 'down_w')]

    nc = _bacc.Bacc("TRN2", target_bir_lowering=False, num_devices=1)
    arrays, args = {}, []
    for name, v in zip(_INS, laid):
        v = _np.ascontiguousarray(v)
        arrays[f"in_{name}_dram"] = v
        args.append(nc.dram_tensor(f"in_{name}_dram", v.shape, mybir.dt.from_np(v.dtype), kind="ExternalInput").ap())
    args.append(nc.dram_tensor("out_dram", (B, S, D), F32, kind="ExternalOutput").ap())
    flamingo_layer(nc, *args)
    r = _run(nc, [arrays], core_ids=[0])
    return r.results[0]["out_dram"]
```

```python
from contextlib import ExitStack

import concourse.bass as bass
from concourse import mybir

P = 128
ALU = mybir.AluOpType
ACT = mybir.ActivationFunctionType
AX = mybir.AxisListType
F32 = mybir.dt.float32
BF16 = mybir.dt.bfloat16
U32 = mybir.dt.uint32
I32 = mybir.dt.int32


def flamingo_layer(nc, x, ctxT, g_xattn, g_ffn, WqT, bq, WkT, bk, WvT, bv, WoT, bo,
                   w_router, fc1_w, fc2_w, gate_w, up_w, down_w, out):
    B, S, D = x.shape
    H = 16
    DK = D // H
    T = B * S
    NT = T // P
    TB = S // P
    DC = D // P
    E = fc1_w.shape[0]
    I2 = fc1_w.shape[2]
    IE = I2 // 2
    ISH = gate_w.shape[1]
    IC = ISH // P
    G = 4
    NG = H // G
    GROUPS = B * NG
    TERMS = 6
    Q_PART = [0, 1, 2, 0, 1, 0]
    K_PART = [0, 0, 0, 1, 1, 2]
    KS = TERMS * DK
    KM = KS + 2
    VW = 2 * DK
    SLOTS = (2 * T + E * (P - 1)) // P
    UN = 3
    assert SLOTS % UN == 0
    PASSES = SLOTS // UN
    EPS = 1e-5

    q_scr = nc.dram_tensor("q_parts", (B, 3, D, S), BF16, kind="Internal").ap()
    k_scr = nc.dram_tensor("k_parts", (B, 3, D, S), BF16, kind="Internal").ap()
    v_scr = nc.dram_tensor("v_rows", (B, TB, P, H * VW), F32, kind="Internal").ap()
    slot_x = nc.dram_tensor("slot_x", (SLOTS * P, D), F32, kind="Internal").ap()
    slot_y = nc.dram_tensor("slot_y", (SLOTS * P, D), F32, kind="Internal").ap()

    with ExitStack() as stack:
        def sb(name, shape, dt=F32):
            return stack.enter_context(nc.sbuf_tensor(name, shape, dt))

        def sem(name):
            return stack.enter_context(nc.semaphore(name))

        def sems(name, n):
            return [sem(f"{name}{i}") for i in range(n)]

        ident = sb("ident", [P, P])
        before = sb("before", [P, P])
        ones = sb("ones", [P, P])
        W = {n: sb(f"w_{n}", [P, DC, D]) for n in "qkvo"}
        wr = sb("wr", [P, DC, E])
        wgate = sb("wgate", [P, DC, ISH])
        wup = sb("wup", [P, DC, ISH])
        wdown = sb("wdown", [P, IC, D])
        fc2 = sb("fc2", [P, IE // P, E, D])
        bias_qk = sb("bias_qk", [P, 2, DC])
        bias_sc = sb("bias_sc", [P, 2, DC])
        bv_row = sb("bv_row", [P, D])
        bo_row = sb("bo_row", [P, D])
        gates = sb("gates", [P, 2])
        tg = sb("tg", [P, 2])
        X = sb("X", [P, NT, D])
        CH = sb("CH", [P, NT, D])
        ZERO = sb("ZERO", [P, D])
        stats = sb("stats", [P, NT, 6])
        mv = sb("mv", [P, NT, 2])
        var_eps = sb("var_eps", [P, NT])
        rstd = sb("rstd", [P, NT])
        minus_half = sb("minus_half", [P, NT])

        R1 = sb("R1", [P, 8192])
        R2 = sb("R2", [P, 8192])
        R3 = sb("R3", [P, 8192])
        R4 = sb("R4", [P, 3072])
        PS = stack.enter_context(nc.psum_tensor("PS", [P, 8, 512], F32))

        fc1 = R3[:, :].rearrange("p (c e n) -> p c e n", c=DC, e=E)
        XN = R2[:, 0:2048].rearrange("p (s t d) -> p s t d", s=2, t=TB)
        XNT = R2[:, 2048:4096].rearrange("p (s c n) -> p s c n", s=2, c=DC)
        CT = R2[:, 4096:6144].rearrange("p (s c n) -> p s c n", s=2, c=DC)
        QF = R2[:, 6144:8192].rearrange("p (j n) -> p j n", j=4)
        VA = R3[:, 0:4096].rearrange("p (s t w) -> p s t w", s=2, t=TB)
        RQ = R3[:, 4096:5120].rearrange("p (j n) -> p j n", j=2)
        QP = R3[:, 5120:8192].bitcast(BF16).rearrange("p (j a n) -> p j a n", j=4, a=3)
        QS = [R1[:, 1024 * g:1024 * (g + 1)].bitcast(BF16).rearrange("p (h n) -> p h n", h=G) for g in range(NG)]
        KST = [R1[:, 4096 + 1024 * g:4096 + 1024 * (g + 1)].bitcast(BF16).rearrange("p (h n) -> p h n", h=G)
               for g in range(NG)]
        PT = R2[:, :].rearrange("p (k h n) -> p k h n", k=TB, h=G)
        VG = [R4[:, 512 * g:512 * (g + 1)].rearrange("p (k w) -> p k w", k=TB) for g in range(NG)]
        OT = [R4[:, 2048 + 512 * i:2048 + 512 * (i + 1)] for i in range(2)]
        nmax = sb("nmax", [P, 2, G * TB])
        mparts = sb("mparts", [G * TB, 2, 2, P], BF16)
        rden = sb("rden", [P, 2, TB, G])
        CTT = R2[:, 0:2048].rearrange("p (s c n) -> p s c n", s=2, c=DC)
        AO = R2[:, 2048:4096].rearrange("p (s n) -> p s n", s=4)
        CTT0 = R1[:, 5120:6144].rearrange("p (c n) -> p c n", c=DC)
        AO0 = R1[:, 4096:5120].rearrange("p (s n) -> p s n", s=2)
        H2T = R1[:, 0:4096].rearrange("p (c n) -> p c n", c=DC)
        SG = R2[:, 4096:5120].rearrange("p (s n) -> p s n", s=2)
        HS = R1[:, 4096:8192].rearrange("p (s c n) -> p s c n", s=2, c=IC)
        XG = R4[:, 0:768].rearrange("p (s d) -> p s d", s=UN)
        XGT = R4[:, 768:1536].rearrange("p (s d) -> p s d", s=UN)
        HE = R4[:, 1536:2304].rearrange("p (s d) -> p s d", s=UN)
        HET = R4[:, 2304:3072].rearrange("p (s d) -> p s d", s=UN)
        SE = R2[:, 5120:5888].rearrange("p (s d) -> p s d", s=UN)
        YE = R2[:, 5888:6656].rearrange("p (s d) -> p s d", s=UN)
        NGA = 8
        GA = R3[:, 0:2 * NGA * D].rearrange("p (s k d) -> p s k d", s=NGA, k=2)
        FO = R3[:, 4096:4096 + NGA * D].rearrange("p (s d) -> p s d", s=NGA)

        LG = sb("LG", [P, NT, E])
        mx8 = sb("mx8", [P, NT, 8])
        ix8 = sb("ix8", [P, NT, 8], U32)
        ixf = sb("ixf", [P, NT, 2])
        io8 = sb("io8", [P, E])
        io16 = sb("io16", [P, NT])
        io40 = sb("io40", [P, SLOTS])
        OH = sb("OH", [P, 3, NT, E])
        CU = sb("CU", [P, 2, NT, E])
        cnt_gt = sb("cnt_gt", [P, E, NT])
        tl = sb("tl", [P, 4, E])
        pos_base = sb("pos_base", [P, NT, E])
        posf = sb("posf", [P, 2, NT])
        pos = sb("pos", [P, 2, NT], U32)
        ge = sb("ge", [P, SLOTS, E])
        eidf = sb("eidf", [P, SLOTS])
        eid = sb("eid", [1, SLOTS], I32)
        sc = sb("sc", [P, 4, NT])
        scg = sb("scg", [P, 2, NT])

        w_in = {n: sem(f"w_in_{n}") for n in ("q", "k", "v", "o", "router", "shared", "fc1", "fc2", "bias", "small")}
        x_in = sems("x_in", B)
        ct_in = sems("ct_in", 2)
        const_ready, consts = sem("const_ready"), sem("consts")
        scaled = sem("scaled")
        ln_stats, ln_mv, ln_ve, ln_rstd = sem("ln_stats"), sem("ln_mv"), sem("ln_ve"), sem("ln_rstd")
        xn_ready, xt_done, xnt_ready = sem("xn_ready"), sem("xt_done"), sem("xnt_ready")
        qk_done, v_done = sem("qk_done"), sem("v_done")
        qf_ready, q1_ready, qr_ready, q2_ready, q3_ready = (sem(n) for n in ("qf_ready", "q1_ready", "qr_ready", "q2_ready", "q3_ready"))
        qp_out, va_out = sems("qp_out", 4), sems("va_out", 2)
        va_ready = sem("va_ready")
        va_ones = sem("va_ones")

        ld_group = sems("ld_group", NG)
        kones = sem("kones")
        smax_done, max_ready = sem("smax_done"), sem("max_ready")
        mt_done, m1_ready, m2_ready = sem("mt_done"), sem("m1_ready"), sem("m2_ready")
        m_in = sems("m_in", 2)
        st_done, exp_done, pv_done, ot_ready = sem("st_done"), sem("exp_done"), sem("pv_done"), sem("ot_ready")
        ot_t, rden_ready, ctx_ready = sem("ot_t"), sem("rden_ready"), sem("ctx_ready")

        ct_t, ctt_ready, wo_done, ao_ready, x1_ready = (sem(n) for n in ("ct_t", "ctt_ready", "wo_done", "ao_ready", "x1_ready"))
        h2_ready, h2_t, h2t_ready, lg_done, lg_ready = (sem(n) for n in ("h2_ready", "h2_t", "h2t_ready", "lg_done", "lg_ready"))
        dve_route, route_pe, exp_sc = sem("dve_route"), sem("route_pe"), sem("exp_sc")
        zero_ready, zero_out, scattered = sem("zero_ready"), sem("zero_out"), sem("scattered")
        gu_done, silu_ready, hs_ready, down_done, base_ready = (sem(n) for n in ("gu_done", "silu_ready", "hs_ready", "down_done", "base_ready"))
        xg_in = sems("xg_in", UN)
        xg_t, xgt_ready, h1_done, se_ready, he_ready, he1 = (sem(n) for n in ("xg_t", "xgt_ready", "h1_done", "se_ready", "he_ready", "he1"))
        he_t, het_ready, y_done, y_ready = (sem(n) for n in ("he_t", "het_ready", "y_done", "y_ready"))
        y_out = sems("y_out", UN)
        ga_in = sems("ga_in", 2 * NGA)
        fo1, fo_ready = sem("fo1"), sem("fo_ready")
        fo_out = sems("fo_out", NGA)

        block = stack.enter_context(nc.Block())

        def wait(eng, s, n):
            if not isinstance(n, int) or n > 0:
                eng.wait_ge(s, n)

        def over_slots(eng, step):
            for it in range(2):
                for u in range(UN):
                    step(it, u, it == 0, False)
            with eng.Fori(2, PASSES - 1) as it:
                for u in range(UN):
                    step(it, u, False, False)
            for u in range(UN):
                step(PASSES - 1, u, False, True)

        EARLY = 4 * G

        def smax_schedule(i, kt):
            s = 4 * i + 6 + kt
            return s if s < GROUPS * G else None

        OUT_AT = TB + 1
        M2_AT = 2 * TB + 2
        ZPIECES = 3
        assert SLOTS % ZPIECES == 0
        BE = B - 1
        COMBINED = (0, 1, 1, 2)
        AHEAD = 2

        def ctt(b, c):
            return CTT[:, b % 2, c, :] if b else CTT0[:, c, :]

        def ctt_bank(b, c):
            return c if b else 4 + c

        def wo_bank(b, h):
            return 2 + h if b else 4 + h

        ROUTE_DIFF = 2 * NT + 2
        ROUTE_OH = ROUTE_DIFF + 3
        ROUTE_POS = ROUTE_OH + 27
        ROUTE_EID = ROUTE_POS + 3

        @block.sync
        def _(sp):
            sp.dma_start(CT[:, 0, :, :], ctxT[:, 0:S].rearrange("(c p) n -> p c n", p=P)).then_inc(ct_in[0], 16)
            sp.dma_start(W["v"][:, :, :], WvT.rearrange("(c p) n -> p c n", p=P)).then_inc(w_in["v"], 16)
            sp.dma_start(W["k"][:, :, :], WkT.rearrange("(c p) n -> p c n", p=P)).then_inc(w_in["k"], 16)
            sp.dma_start(W["q"][:, :, :], WqT.rearrange("(c p) n -> p c n", p=P)).then_inc(w_in["q"], 16)
            sp.dma_start(CT[:, 1, :, :], ctxT[:, S:2 * S].rearrange("(c p) n -> p c n", p=P)).then_inc(ct_in[1], 16)
            for b in range(2, B):
                sp.dma_start(X[:, b * TB:(b + 1) * TB, :], x[b].rearrange("(t p) d -> p t d", p=P)).then_inc(x_in[b], 16)
            sp.dma_start(W["o"][:, :, :], WoT.rearrange("(c p) n -> p c n", p=P)).then_inc(w_in["o"], 16)
            def store_parts(b):
                sp.wait_ge(va_ready, TB * (b + 1))
                sp.dma_start(v_scr[b].rearrange("t p w -> p t w"), VA[:, b % 2, :, :]).then_inc(va_out[b % 2], 16)
                for j in range(4):
                    dst = k_scr if j < 2 else q_scr
                    sp.wait_ge(q1_ready, 4 * b + j + 1)
                    sp.wait_ge(q3_ready, 4 * b + j + 1)
                    sp.dma_start(dst[b, :, (j % 2) * P:(j % 2 + 1) * P, :].rearrange("a p n -> p a n"), QP[:, j, :, :])\
                      .then_inc(qp_out[j], 16)

            def parts_stored(b):
                for j in range(4):
                    sp.wait_ge(qp_out[j], 16 * (b + 1))
                sp.wait_ge(va_out[b % 2], 16 * (b // 2 + 1))

            def load_group(i):
                b, g = divmod(i, NG)
                if i >= NG:
                    sp.wait_ge(pv_done, TB * (i - NG + 1))
                rows = slice(g * G * DK, (g + 1) * G * DK)
                for t in range(TERMS):
                    sp.dma_start(QS[g][t * DK:(t + 1) * DK, :, :],
                                 q_scr[b, Q_PART[t], rows, :].rearrange("(h d) n -> d h n", h=G)).then_inc(ld_group[g], 16)
                    sp.dma_start(KST[g][t * DK:(t + 1) * DK, :, :],
                                 k_scr[b, K_PART[t], rows, :].rearrange("(h d) n -> d h n", h=G)).then_inc(ld_group[g], 16)
                sp.dma_start(VG[g][:, :, :], v_scr[b, :, :, g * G * VW:(g + 1) * G * VW].rearrange("t p w -> p t w"))\
                  .then_inc(ld_group[g], 16)

            def load_max(i):
                for part, s in ((0, m1_ready), (1, m2_ready)):
                    sp.wait_ge(s, i + 1)
                    sp.dma_start(QS[i % NG][KS + part:KS + part + 1, :, :].rearrange("p h n -> p (h n)"),
                                 mparts[:, i % 2, part, :]).then_inc(m_in[i % 2], 16)

            store_parts(0)
            parts_stored(0)
            load_group(0)
            store_parts(1)
            load_group(1)
            store_parts(2)
            load_group(2)
            store_parts(3)
            load_max(0)
            for b in range(1, B):
                parts_stored(b)
            for i in range(GROUPS):
                if i + 3 < GROUPS:
                    load_group(i + 3)
                if i + 1 < GROUPS:
                    load_max(i + 1)
                if i == 1:
                    for t_, src in ((wgate, gate_w), (wup, up_w), (wdown, down_w)):
                        sp.dma_start(t_[:, :, :], src.rearrange("(c p) n -> p c n", p=P)).then_inc(w_in["shared"], 16)
                    sp.dma_start(wr[:, :, :], w_router.rearrange("(c p) n -> p c n", p=P)).then_inc(w_in["router"], 16)
                if 2 <= i < 2 + E // 2:
                    e = slice(2 * (i - 2), 2 * (i - 1))
                    for c in range(DC):
                        sp.dma_start(fc1[:, c, e, :], fc1_w[e, c * P:(c + 1) * P, :].rearrange("e p n -> p e n"))\
                          .then_inc(w_in["fc1"], 16)
                    for c in range(IE // P):
                        sp.dma_start(fc2[:, c, e, :], fc2_w[e, c * P:(c + 1) * P, :].rearrange("e p n -> p e n"))\
                          .then_inc(w_in["fc2"], 16)
                if 2 + E // 2 <= i < 2 + E // 2 + ZPIECES:
                    n = (i - 2 - E // 2) * (SLOTS // ZPIECES)
                    sp.wait_ge(zero_ready, 1)
                    sp.dma_start(slot_x[n * P:(n + SLOTS // ZPIECES) * P, :].rearrange("(n p) d -> p n d", p=P),
                                 ZERO[:, :].unsqueeze(1).to_broadcast([P, SLOTS // ZPIECES, D])).then_inc(zero_out, 16)
            sp.wait_ge(scattered, 16 * 2 * NT)
            for u in range(UN):
                sp.dma_start(XG[:, u, :], slot_x[u * P:(u + 1) * P, :]).then_inc(xg_in[u], 16)

            def slot_dmas(it, u, first, last):
                j = it * UN + u
                if not last:
                    sp.wait_ge(xg_t, j + 1)
                    sp.dma_start(XG[:, u, :], slot_x[bass.ds((j + UN) * P, P), :]).then_inc(xg_in[u], 16)
                if not (first and u < 2):
                    store_result(j - 2, (u - 2) % UN)

            def store_result(j, u):
                sp.wait_ge(y_ready, j + 1)
                sp.dma_start(slot_y[bass.ds(j * P, P), :], YE[:, u, :]).then_inc(y_out[u], 16)

            over_slots(sp, slot_dmas)
            for j in (SLOTS - 2, SLOTS - 1):
                store_result(j, j % UN)
            for t in range(NT):
                b, q = divmod(t, TB)
                sp.wait_ge(fo_ready, t + 1)
                sp.dma_start(out[b, q * P:(q + 1) * P, :], FO[:, t % NGA, :]).then_inc(fo_out[t % NGA], 16)
            for n in range(NGA):
                sp.wait_ge(fo_out[n], 16 * (NT // NGA))

        @block.gpsimd
        def _(pool):
            nc.gpsimd.memset(ident[:, :], 0.0).then_inc(const_ready, 1)
            nc.gpsimd.memset(before[:, :], 1.0).then_inc(const_ready, 1)
            nc.gpsimd.memset(ones[:, :], 1.0).then_inc(consts, 1)
            nc.gpsimd.memset(minus_half[:, :], -0.5).then_inc(consts, 1)
            nc.gpsimd.memset(ZERO[:, :], 0.0).then_inc(zero_ready, 1)
            pool.wait_ge(const_ready, 2)
            nc.gpsimd.affine_select(out=ident[:, :], in_=ident[:, :], compare_op=ALU.not_equal, fill=1.0, base=0,
                                    pattern=[[-1, P]], channel_multiplier=1).then_inc(consts, 1)
            nc.gpsimd.affine_select(out=before[:, :], in_=before[:, :], compare_op=ALU.is_gt, fill=0.0, base=0,
                                    pattern=[[1, P]], channel_multiplier=-1).then_inc(consts, 1)
            nc.gpsimd.iota(io8[:, :], [[1, E]], base=0, channel_multiplier=0,
                           allow_small_or_imprecise_dtypes=True).then_inc(consts, 1)
            nc.gpsimd.iota(io16[:, :], [[P, NT]], base=0, channel_multiplier=0,
                           allow_small_or_imprecise_dtypes=True).then_inc(consts, 1)
            nc.gpsimd.iota(io40[:, :], [[1, SLOTS]], base=0, channel_multiplier=0,
                           allow_small_or_imprecise_dtypes=True).then_inc(consts, 1)
            nc.gpsimd.memset(VA[:, :, :, :], 1.0).then_inc(va_ones, 1)
            pool.wait_ge(va_ones, 1)
            for b in range(B):
                pool.wait_ge(ln_ve, b + 1)
                sl = slice(b * TB, (b + 1) * TB)
                nc.gpsimd.tensor_tensor(rstd[:, sl], var_eps[:, sl], minus_half[:, sl], ALU.pow).then_inc(ln_rstd, 1)
            for g in range(NG):
                pool.wait_ge(kones, g) if g else pool.wait_ge(ln_rstd, B)
                nc.gpsimd.memset(KST[g][KS:KM, :, :], 1.0).then_inc(kones, 1)
            pool.wait_ge(kones, NG)
            for b in range(B):
                pool.wait_ge(ln_ve, B + b + 1)
                sl = slice(b * TB, (b + 1) * TB)
                nc.gpsimd.tensor_tensor(rstd[:, sl], var_eps[:, sl], minus_half[:, sl], ALU.pow).then_inc(ln_rstd, 1)
            pool.wait_ge(dve_route, ROUTE_POS)
            pool.wait_ge(zero_out, 16 * ZPIECES)
            for t in range(NT):
                for k in range(2):
                    nc.gpsimd.indirect_dma_start(slot_x, bass.IndirectOffsetOnAxis(ap=pos[:, k, t:t + 1], axis=0),
                                                 CH[:, t, :], None).then_inc(scattered, 16)
            for u in range(UN):
                pool.wait_ge(y_out[u], 16 * (SLOTS // UN))
            for t in range(NT):
                for k in range(2):
                    if t >= NGA:
                        pool.wait_ge(fo_ready, t - NGA + 1)
                    nc.gpsimd.indirect_dma_start(GA[:, t % NGA, k, :], None, slot_y,
                                                 bass.IndirectOffsetOnAxis(ap=pos[:, k, t:t + 1], axis=0))\
                        .then_inc(ga_in[2 * (t % NGA) + k], 16)

        @block.scalar
        def _(act):
            act.dma_start(X[:, 0:TB, :], x[0].rearrange("(t p) d -> p t d", p=P)).then_inc(x_in[0], 16)
            for t_, src in ((bias_qk[:, 0, :], bq), (bias_qk[:, 1, :], bk), (bv_row[:, :], bv.partition_broadcast(P))):
                act.dma_start(t_, src).then_inc(w_in["bias"], 16)
            act.dma_start(X[:, TB:2 * TB, :], x[1].rearrange("(t p) d -> p t d", p=P)).then_inc(x_in[1], 16)
            for t_, src in ((gates[:, 0:1], g_xattn), (gates[:, 1:2], g_ffn), (bo_row[:, :], bo)):
                act.dma_start(t_, src.partition_broadcast(P)).then_inc(w_in["small"], 16)
            act.wait_ge(w_in["bias"], 48)
            nc.scalar.activation(bias_sc[:, 0, :], bias_qk[:, 0, :], ACT.Copy, scale=0.25).then_inc(scaled, 1)
            nc.scalar.activation(bias_sc[:, 1, :], bias_qk[:, 1, :], ACT.Copy).then_inc(scaled, 1)
            act.wait_ge(scaled, 2)
            def xnt_copy(b):
                if b >= 2:
                    act.wait_ge(qk_done, 4 * (b - 1))
                for c in range(DC):
                    act.wait_ge(xt_done, 2 * b + c + 1)
                    nc.scalar.copy(XNT[:, b % 2, c, :], PS[:, c, :]).then_inc(xnt_ready, 1)

            for b in range(B):
                for j in range(4):
                    if j == 1 and b == 0:
                        xnt_copy(0)
                    if j == (2 if b else 3) and b + 1 < B:
                        xnt_copy(b + 1)
                    act.wait_ge(qk_done, 4 * b + j + 1)
                    if j == 1 and b + 2 < B:
                        act.wait_ge(v_done, 2 * (b + 1))
                        act.dma_start(CT[:, b % 2, :, :], ctxT[:, (b + 2) * S:(b + 3) * S]
                                      .rearrange("(c p) n -> p c n", p=P)).then_inc(ct_in[b % 2], 16)
                    if b:
                        act.wait_ge(qr_ready, 4 * (b - 1) + j + 1)
                    bias = bias_sc[:, 1 - j // 2, j % 2:j % 2 + 1]
                    scale = 1.0 if j < 2 else 0.25
                    nc.scalar.activation(QF[:, j, :], PS[:, 2 + j % 2, :], ACT.Identity, bias=bias, scale=scale).then_inc(qf_ready, 1)
                    if b:
                        act.wait_ge(qp_out[j], 16 * b)
                    nc.scalar.activation(QP[:, j, 0, :], PS[:, 2 + j % 2, :], ACT.Identity, bias=bias, scale=scale).then_inc(q1_ready, 1)
            act.wait_ge(w_in["small"], 48)
            nc.scalar.activation(tg[:, :], gates[:, :], ACT.Tanh).then_inc(scaled, 1)
            def m_first(i):
                act.wait_ge(mt_done, i + 1)
                if i >= 2:
                    act.wait_ge(m_in[i % 2], 32 * (i // 2))
                nc.scalar.copy(mparts[:, i % 2, 0, :], PS[0:G * TB, 7, 0:P]).then_inc(m1_ready, 1)

            def out_copy(i):
                act.wait_ge(pv_done, TB * (i + 1))
                if i >= 2:
                    act.wait_ge(ot_t, i - 1)
                nc.scalar.copy(OT[i % 2], PS[:, 6, :]).then_inc(ot_ready, 1)

            for i in range(GROUPS):
                if i == 0:
                    m_first(0)
                for kt in range(TB):
                    for j in range(G):
                        act.wait_ge(st_done, G * (TB * i + kt) + j + 1)
                        if i:
                            act.wait_ge(pv_done, TB * (i - 1) + kt + 1)
                        nc.scalar.activation(PT[:, kt, j, :], PS[:, j, :], ACT.Exp).then_inc(exp_done, 1)
                        if j == 2 and kt == 0 and i:
                            out_copy(i - 1)
                        if j == 2 and kt == 2 and i + 1 < GROUPS:
                            m_first(i + 1)
            out_copy(GROUPS - 1)
            def ctt_first(b):
                act.wait_ge(ct_t, 2 * b + 1)
                if b >= 2:
                    act.wait_ge(wo_done, 2 * (b - 1))
                nc.scalar.copy(CTT[:, b % 2, 0, :], PS[:, 0, :]).then_inc(ctt_ready, 1)

            def h2t_first(b):
                act.wait_ge(h2_t, 2 * b + 1)
                nc.scalar.copy(H2T[:, 0, b * S:(b + 1) * S], PS[:, 4, :]).then_inc(h2t_ready, 1)

            def silu(b, c):
                n = IC * b + c
                act.wait_ge(gu_done, n + 1)
                if n >= 2:
                    act.wait_ge(hs_ready, n - 1)
                nc.scalar.activation(SG[:, n % 2, :], PS[:, 2 * (n % 2), :], ACT.Silu).then_inc(silu_ready, 1)

            for b in range(B):
                if b:
                    h2t_first(b - 1)
                if b + 1 < B:
                    ctt_first(b + 1)
            for c in range(AHEAD):
                silu(0, c)
            h2t_first(B - 1)
            for c in range(AHEAD, IC):
                silu(0, c)
            for b in range(1, BE):
                for c in range(IC):
                    silu(b, c)
                if b == 1:
                    act.wait_ge(dve_route, ROUTE_DIFF)
                    nc.scalar.activation(sc[:, 1, :], sc[:, 0, :], ACT.Exp).then_inc(exp_sc, 1)
            act.wait_ge(xg_t, 1)
            nc.scalar.copy(XGT[:, 0, :], PS[:, 0, 0:D]).then_inc(xgt_ready, 1)

            def hidden_copy(j, u):
                act.wait_ge(he_t, j + 1)
                nc.scalar.copy(HET[:, u, :], PS[:, 4, 0:IE]).then_inc(het_ready, 1)

            def slot_acts(it, u, first, last):
                j = it * UN + u
                act.wait_ge(h1_done, j + 1)
                wait(act, he_ready, j - UN + 1)
                nc.scalar.activation(SE[:, u, :], PS[:, 1 + u, 0:IE], ACT.Silu).then_inc(se_ready, 1)
                if not (last and u == UN - 1):
                    act.wait_ge(xg_t, j + 2)
                    nc.scalar.copy(XGT[:, (u + 1) % UN, :], PS[:, 0, 0:D]).then_inc(xgt_ready, 1)
                if not (first and u == 0):
                    hidden_copy(j - 1, (u - 1) % UN)

            over_slots(act, slot_acts)
            hidden_copy(SLOTS - 1, UN - 1)
            for b in range(BE, B):
                for c in range(IC):
                    silu(b, c)

        @block.vector
        def _(dve):

            def layernorm(b, n0):
                sl = slice(b * TB, (b + 1) * TB)
                for t in range(TB):
                    nc.vector.bn_stats(stats[:, b * TB + t, :], X[:, b * TB + t, :]).then_inc(ln_stats, 1)
                dve.wait_ge(ln_stats, 4 * (n0 + b + 1))
                for t in range(TB):
                    nc.vector.bn_aggr(mv[:, b * TB + t, :], stats[:, b * TB + t, :]).then_inc(ln_mv, 1)
                dve.wait_ge(ln_mv, 4 * (n0 + b + 1))
                nc.vector.tensor_scalar(var_eps[:, sl], mv[:, sl, 1], EPS, None, ALU.add).then_inc(ln_ve, 1)

            def normalise(b, n0, dst, ready):
                dve.wait_ge(ln_rstd, n0 + b + 1)
                for t in range(TB):
                    tt = b * TB + t
                    nc.vector.tensor_scalar(dst(t), X[:, tt, :], mv[:, tt, 0:1], rstd[:, tt:tt + 1],
                                            ALU.subtract, ALU.mult).then_inc(ready, 1)

            def one_max(n):
                s, qt = divmod(n, TB)
                i, j = divmod(s, G)
                dve.wait_ge(smax_done, n + 1)
                if n % 16 == 0 and i >= 2:
                    dve.wait_ge(mt_done, i - 1)
                nc.vector.tensor_reduce(nmax[:, i % 2, j * TB + qt:j * TB + qt + 1], PS[:, 4 + n % 2, :], AX.X,
                                        ALU.max, negate=True).then_inc(max_ready, 1)

            early = iter(range(EARLY))

            def early_max(b):
                if b >= 3:
                    n = next(early, None)
                    if n is not None:
                        one_max(n)

            dve.wait_ge(x_in[0], 16)
            layernorm(0, 0)
            dve.wait_ge(w_in["bias"], 48)
            dve.wait_ge(va_ones, 1)
            for b in range(B):
                s = b % 2
                if 0 < b < B - 1:
                    dve.wait_ge(xt_done, 2 * b)
                    normalise(b + 1, 0, lambda t: XN[:, (b + 1) % 2, t, :], xn_ready)
                if b >= 2:
                    dve.wait_ge(va_out[s], 16 * (b // 2))
                for t in range(TB):
                    dve.wait_ge(v_done, 2 * b + t // 2 + 1)
                    nc.vector.tensor_tensor(
                        VA[:, s, t, :].rearrange("p (h w) -> p h w", w=VW)[:, :, 0:DK],
                        PS[:, 6 + t // 2, (t % 2) * D:(t % 2 + 1) * D].rearrange("p (h w) -> p h w", w=DK),
                        bv_row[:, :].rearrange("p (h w) -> p h w", w=DK), ALU.add).then_inc(va_ready, 1)
                    early_max(b)
                if b == 0:
                    normalise(0, 0, lambda t: XN[:, 0, t, :], xn_ready)
                for j in range(4):
                    n = 4 * b + j
                    if j == 1 and b == 0:
                        dve.wait_ge(x_in[1], 16)
                        layernorm(1, 0)
                        normalise(1, 0, lambda t: XN[:, 1, t, :], xn_ready)
                    dve.wait_ge(qf_ready, n + 1)
                    dve.wait_ge(q1_ready, n + 1)
                    if n >= 2:
                        dve.wait_ge(q3_ready, n - 1)
                    nc.vector.tensor_tensor(RQ[:, n % 2, :], QF[:, j, :], QP[:, j, 0, :], ALU.subtract).then_inc(qr_ready, 1)
                    dve.wait_ge(qr_ready, n + 1)
                    if b:
                        dve.wait_ge(qp_out[j], 16 * b)
                    nc.vector.tensor_copy(QP[:, j, 1, :], RQ[:, n % 2, :]).then_inc(q2_ready, 1)
                    early_max(b)
                    dve.wait_ge(q2_ready, n + 1)
                    nc.vector.tensor_tensor(QP[:, j, 2, :], RQ[:, n % 2, :], QP[:, j, 1, :], ALU.subtract).then_inc(q3_ready, 1)
                if b + 2 < B:
                    dve.wait_ge(x_in[b + 2], 16)
                    layernorm(b + 2, 0)

            def head_max(s):
                for qt in range(TB):
                    one_max(TB * s + qt)

            def m_second(i):
                dve.wait_ge(m1_ready, i + 1)
                nc.vector.tensor_tensor(mparts[:, i % 2, 1, :], PS[0:G * TB, 7, 0:P], mparts[:, i % 2, 0, :],
                                        ALU.subtract).then_inc(m2_ready, 1)

            def denominators(i):
                dve.wait_ge(ot_t, i + 1)
                if i >= 2:
                    dve.wait_ge(ctx_ready, TB * (i - 1))
                o = PS[:, 7, :].rearrange("p (q h w) -> p q h w", q=TB, h=G)
                nc.vector.reciprocal(rden[:, i % 2, :, :], o[:, :, :, DK]).then_inc(rden_ready, 1)

            def head_out(i, qt):
                b, g = divmod(i, NG)
                dve.wait_ge(rden_ready, i + 1)
                o = PS[:, 7, qt * P:(qt + 1) * P].rearrange("p (h w) -> p h w", h=G)
                nc.vector.tensor_tensor(
                    CH[:, b * TB + qt, g * G * DK:(g + 1) * G * DK].rearrange("p (h w) -> p h w", h=G),
                    o[:, :, 0:DK], rden[:, i % 2, qt, :].unsqueeze(2).to_broadcast([P, G, DK]),
                    ALU.mult).then_inc(ctx_ready, 1)

            dve.wait_ge(w_in["small"], 48)
            dve.wait_ge(scaled, 3)

            def ctt_second(b):
                dve.wait_ge(ct_t, 2 * b + 2)
                if b >= 2:
                    dve.wait_ge(wo_done, 2 * (b - 1))
                for c in range(DC) if b == 0 else (1,):
                    nc.vector.tensor_copy(ctt(b, c), PS[:, ctt_bank(b, c), :]).then_inc(ctt_ready, 1)

            def ao(n):
                return AO[:, n % 4, :] if n >= 2 else AO0[:, n, :]

            def residual(b):
                for h in range(2):
                    n = 2 * b + h
                    dve.wait_ge(wo_done, n + 1)
                    if n >= 4:
                        dve.wait_ge(x1_ready, n - 3)
                    tt = slice(b * TB + 2 * h, b * TB + 2 * h + 2)
                    nc.vector.tensor_tensor(ao(n).rearrange("p (t d) -> p t d", t=2),
                                            PS[:, wo_bank(b, h), :].rearrange("p (t d) -> p t d", t=2),
                                            bo_row[:, :].unsqueeze(1).to_broadcast([P, 2, D]), ALU.add).then_inc(ao_ready, 1)
                    dve.wait_ge(ao_ready, n + 1)
                    nc.vector.scalar_tensor_tensor(out=X[:, tt, :], in0=ao(n).rearrange("p (t d) -> p t d", t=2),
                                                   scalar=tg[:, 0:1], in1=X[:, tt, :], op0=ALU.mult, op1=ALU.add)\
                        .then_inc(x1_ready, 1)

            def statistics(b):
                dve.wait_ge(x1_ready, 2 * b + 2)
                layernorm(b, B)

            for n in early:
                one_max(n)
            m_second(0)
            for n in range(EARLY, 6 * TB):
                one_max(n)
            for i in range(GROUPS):
                for kt in range(TB):
                    s = smax_schedule(i, kt)
                    for qt in range(TB):
                        if s is not None:
                            one_max(TB * s + qt)
                        if i:
                            n = TB * kt + qt - OUT_AT
                            if n == 0:
                                denominators(i - 1)
                            elif 0 < n <= TB:
                                head_out(i - 1, n - 1)
                        if TB * kt + qt == M2_AT and i + 1 < GROUPS:
                            m_second(i + 1)
            ctt_second(0)
            residual(0)
            statistics(0)
            denominators(GROUPS - 1)
            for qt in range(TB):
                head_out(GROUPS - 1, qt)

            def h2t_second(b):
                dve.wait_ge(h2_t, 2 * b + 2)
                nc.vector.tensor_copy(H2T[:, 1, b * S:(b + 1) * S], PS[:, 5, :]).then_inc(h2t_ready, 1)

            def logits(b):
                dve.wait_ge(lg_done, b + 1)
                nc.vector.tensor_copy(LG[:, b * TB:(b + 1) * TB, :],
                                      PS[:, 6, 0:TB * E].rearrange("p (t e) -> p t e", t=TB)).then_inc(lg_ready, 1)

            def hidden(b, c):
                n = IC * b + c
                dve.wait_ge(silu_ready, n + 1)
                if b >= 2:
                    dve.wait_ge(down_done, 2 * (b - 1))
                nc.vector.tensor_tensor(HS[:, b % 2, c, :], SG[:, n % 2, :], PS[:, 2 * (n % 2) + 1, :], ALU.mult)\
                    .then_inc(hs_ready, 1)

            def shared_out(b, h):
                dve.wait_ge(down_done, 2 * b + h + 1)
                tt = slice(b * TB + 2 * h, b * TB + 2 * h + 2)
                nc.vector.scalar_tensor_tensor(out=X[:, tt, :], in0=PS[:, 6 + h, :].rearrange("p (t d) -> p t d", t=2),
                                               scalar=tg[:, 1:2], in1=X[:, tt, :], op0=ALU.mult, op1=ALU.add)\
                    .then_inc(base_ready, 1)

            for b in range(B):
                if b:
                    residual(b)
                    h2t_second(b - 1)
                if b + 1 < B:
                    ctt_second(b + 1)
                if b:
                    statistics(b)
                if b:
                    logits(b - 1)
                normalise(b, B, lambda t: CH[:, b * TB + t, :], h2_ready)
            for c in range(AHEAD):
                hidden(0, c)
            h2t_second(B - 1)
            hidden(0, AHEAD)
            logits(B - 1)

            chain = [0]

            def step(ins):
                chain[0] += 1
                ins.then_inc(dve_route, 1)
                dve.wait_ge(dve_route, chain[0])

            def many(instructions):
                for ins in instructions:
                    chain[0] += 1
                    ins.then_inc(dve_route, 1)
                dve.wait_ge(dve_route, chain[0])

            dve.wait_ge(lg_ready, B)
            dve.wait_ge(consts, 7)
            many(nc.vector.max(mx8[:, t, :], LG[:, t, :]) for t in range(NT))
            many(nc.vector.max_index(ix8[:, t, :], mx8[:, t, :], LG[:, t, :]) for t in range(NT))
            step(nc.vector.tensor_copy(ixf[:, :, :], ix8[:, :, 0:2]))
            step(nc.vector.tensor_tensor(sc[:, 0, :], mx8[:, :, 1], mx8[:, :, 0], ALU.subtract))
            assert chain[0] == ROUTE_DIFF
            for k in range(2):
                step(nc.vector.tensor_tensor(OH[:, k, :, :], io8[:, :].unsqueeze(1).to_broadcast([P, NT, E]),
                                             ixf[:, :, k].unsqueeze(2).to_broadcast([P, NT, E]), ALU.is_equal))
            step(nc.vector.tensor_tensor(OH[:, 2, :, :], OH[:, 0, :, :], OH[:, 1, :, :], ALU.add))
            assert chain[0] == ROUTE_OH
            for c in range(AHEAD + 1, IC):
                hidden(0, c)
            dve.wait_ge(route_pe, 2)
            tot = PS[:, 5, 0:NT * E].rearrange("p (t e) -> p t e", t=NT)
            rank = PS[:, 4, 0:NT * E].rearrange("p (t e) -> p t e", t=NT)
            step(nc.vector.tensor_copy(CU[:, 0, :, :], tot))
            a = 0
            for d in (1, 2, 4, 8):
                many([nc.vector.tensor_copy(CU[:, 1 - a, 0:d, :], CU[:, a, 0:d, :]),
                      nc.vector.tensor_tensor(CU[:, 1 - a, d:NT, :], CU[:, a, d:NT, :], CU[:, a, 0:NT - d, :], ALU.add)])
                a = 1 - a
            step(nc.vector.tensor_tensor(cnt_gt[:, :, :], CU[:, a, NT - 1, :].unsqueeze(2).to_broadcast([P, E, NT]),
                                         io16[:, :].unsqueeze(1).to_broadcast([P, E, NT]), ALU.is_gt))
            step(nc.vector.tensor_reduce(tl[:, 0, :], cnt_gt[:, :, :], AX.X, ALU.add))
            src = 0
            for n, d in enumerate((1, 2, 4)):
                to = n + 1
                many([nc.vector.tensor_copy(tl[:, to, 0:d], tl[:, src, 0:d]),
                      nc.vector.tensor_tensor(tl[:, to, d:E], tl[:, src, d:E], tl[:, src, 0:E - d], ALU.add)])
                src = to
            step(nc.vector.tensor_tensor(pos_base[:, :, :], CU[:, a, :, :], rank, ALU.add))
            step(nc.vector.tensor_tensor(CU[:, 1 - a, :, :], pos_base[:, :, :], tot, ALU.subtract))
            step(nc.vector.tensor_tensor(tl[:, 1, :], tl[:, 3, :], tl[:, 0, :], ALU.subtract))
            step(nc.vector.tensor_scalar(tl[:, 2, :], tl[:, 1, :], float(P), None, ALU.mult))
            step(nc.vector.tensor_tensor(pos_base[:, :, :], CU[:, 1 - a, :, :],
                                         tl[:, 2, :].unsqueeze(1).to_broadcast([P, NT, E]), ALU.add))
            for k in range(2):
                step(nc.vector.tensor_tensor(CU[:, k, :, :], OH[:, k, :, :], pos_base[:, :, :], ALU.mult))
                step(nc.vector.tensor_reduce(posf[:, k, :], CU[:, k, :, :], AX.X, ALU.add))
            step(nc.vector.tensor_copy(pos[:, :, :], posf[:, :, :]))
            assert chain[0] == ROUTE_POS, chain[0]
            step(nc.vector.tensor_tensor(ge[:, :, :], io40[:, :].unsqueeze(2).to_broadcast([P, SLOTS, E]),
                                         tl[:, 3, :].unsqueeze(1).to_broadcast([P, SLOTS, E]), ALU.is_ge))
            step(nc.vector.tensor_reduce(eidf[:, :], ge[:, :, :], AX.X, ALU.add))
            step(nc.vector.tensor_scalar(eid[:, :], eidf[0:1, :], float(E - 1), None, ALU.min))
            assert chain[0] == ROUTE_EID, chain[0]
            for h in range(2):
                shared_out(0, h)
            for b in range(1, BE):
                for c in range(IC):
                    hidden(b, c)
                for h in range(2):
                    shared_out(b, h)
            dve.wait_ge(exp_sc, 1)
            step(nc.vector.tensor_scalar(sc[:, 2, :], sc[:, 1, :], 1.0, None, ALU.add))
            step(nc.vector.reciprocal(sc[:, 3, :], sc[:, 2, :]))
            step(nc.vector.tensor_tensor(sc[:, 0, :], sc[:, 1, :], sc[:, 3, :], ALU.mult))
            step(nc.vector.tensor_scalar(scg[:, 0, :], sc[:, 3, :], tg[:, 1:2], None, ALU.mult))
            step(nc.vector.tensor_scalar(scg[:, 1, :], sc[:, 0, :], tg[:, 1:2], None, ALU.mult))

            def slot_result(it, u):
                dve.wait_ge(y_done, it * UN + u + 1)
                wait(dve, y_out[u], it * 16)
                nc.vector.tensor_copy(YE[:, u, :], PS[:, 5 + u, 0:D]).then_inc(y_ready, 1)

            def slot_products(it, u, first, last):
                j = it * UN + u
                dve.wait_ge(se_ready, j + 1)
                wait(dve, he_t, j - UN + 1)
                nc.vector.tensor_tensor(HE[:, u, :], SE[:, u, :], PS[:, 1 + u, IE:I2], ALU.mult).then_inc(he_ready, 1)
                if u == UN - 1:
                    slot_result(it, 0)
                elif not first:
                    slot_result(it - 1, u + 1)

            over_slots(dve, slot_products)
            for u in (1, 2):
                slot_result(PASSES - 1, u)
            def combine(t):
                n = t % NGA
                dve.wait_ge(ga_in[2 * n], 16 * (t // NGA + 1))
                dve.wait_ge(ga_in[2 * n + 1], 16 * (t // NGA + 1))
                dve.wait_ge(base_ready, 2 * (t // TB + 1))
                nc.vector.scalar_tensor_tensor(out=X[:, t, :], in0=GA[:, n, 0, :], scalar=scg[:, 0, t:t + 1],
                                               in1=X[:, t, :], op0=ALU.mult, op1=ALU.add).then_inc(fo1, 1)
                dve.wait_ge(fo1, t + 1)
                if t >= NGA:
                    dve.wait_ge(fo_out[n], 16 * (t // NGA))
                nc.vector.scalar_tensor_tensor(out=FO[:, n, :], in0=GA[:, n, 1, :], scalar=scg[:, 1, t:t + 1],
                                               in1=X[:, t, :], op0=ALU.mult, op1=ALU.add).then_inc(fo_ready, 1)

            done = iter(range(NT))
            for c, tiles in zip(range(IC), COMBINED):
                hidden(B - 1, c)
                for _ in range(tiles):
                    combine(next(done))
            for h in range(2):
                shared_out(B - 1, h)
                combine(next(done))
            for t in done:
                combine(t)

        @block.tensor
        def _(pe):
            mm = nc.tensor.matmul
            pe.wait_ge(consts, 3)
            def rows_transpose(b):
                for c in range(DC):
                    pe.wait_ge(xn_ready, TB * (b + 1))
                    if b:
                        pe.wait_ge(xnt_ready, 2 * b)
                    for t in range(TB):
                        last = nc.tensor.transpose(PS[:, c, t * P:(t + 1) * P], XN[:, b % 2, t, c * P:(c + 1) * P], ident[:, :])
                    last.then_inc(xt_done, 1)

            def scores_for_max(n):
                s, qt = divmod(n, TB)
                i, j = divmod(s, G)
                b, g = divmod(i, NG)
                if j == 0 and qt == 0:
                    pe.wait_ge(ld_group[g], 16 * (2 * TERMS + 1) * (b + 1))
                if n >= 2:
                    pe.wait_ge(max_ready, n - 1)
                mm(PS[:, 4 + n % 2, :], QS[g][0:KS, j, qt * P:(qt + 1) * P], KST[g][0:KS, j, :],
                   start=True, stop=True).then_inc(smax_done, 1)

            early = iter(range(EARLY))

            def early_scores(b):
                if b >= 3:
                    n = next(early, None)
                    if n is not None:
                        scores_for_max(n)

            for b in range(B):
                s = b % 2
                pe.wait_ge(w_in["v"], 16)
                pe.wait_ge(ct_in[s], 16 * (b // 2 + 1))
                for t in range(TB):
                    if b:
                        pe.wait_ge(va_ready, TB * b)
                    for c in range(DC):
                        last = mm(PS[:, 6 + t // 2, (t % 2) * D:(t % 2 + 1) * D], CT[:, s, c, t * P:(t + 1) * P],
                                  W["v"][:, c, :], start=(c == 0), stop=(c == DC - 1))
                    if t % 2:
                        last.then_inc(v_done, 1)
                    early_scores(b)
                for j in range(4):
                    n = 4 * b + j
                    if j == 1 and b == 0:
                        rows_transpose(0)
                    if j == (2 if b else 3) and b + 1 < B:
                        rows_transpose(b + 1)
                    if j == 2:
                        pe.wait_ge(xnt_ready, 2 * (b + 1))
                    if n >= 2:
                        pe.wait_ge(q1_ready, n - 1)
                    pe.wait_ge(w_in["k" if j < 2 else "q"], 16)
                    w, src = (W["k"], CT) if j < 2 else (W["q"], XNT)
                    for c in range(DC):
                        last = mm(PS[:, 2 + j % 2, :], w[:, c, (j % 2) * P:(j % 2 + 1) * P], src[:, s, c, :],
                                  start=(c == 0), stop=(c == DC - 1))
                    last.then_inc(qk_done, 1)
                    early_scores(b)

            def max_transpose(i):
                pe.wait_ge(max_ready, TB * G * (i + 1))
                if i == 0:
                    pe.wait_ge(va_ready, TB * B)
                if i >= 2:
                    pe.wait_ge(ctx_ready, TB * (i - 1))
                nc.tensor.transpose(PS[0:G * TB, 7, 0:P], nmax[:, i % 2, :], ident[:, :]).then_inc(mt_done, 1)

            def values(i, kt):
                g = i % NG
                pe.wait_ge(exp_done, G * (TB * i + kt + 1))
                if kt == 0 and i:
                    pe.wait_ge(ot_ready, i)
                if kt == 0 and i == 0:
                    pe.wait_ge(va_ready, TB * B)
                for j in range(G):
                    last = mm(PS[32 * j:32 * j + VW, 6, :], VG[g][:, kt, j * VW:(j + 1) * VW], PT[:, kt, j, :],
                              start=(kt == 0), stop=(kt == TB - 1), tile_position=(0, 32 * j))
                last.then_inc(pv_done, 1)

            def out_transpose(i):
                pe.wait_ge(ot_ready, i + 1)
                pe.wait_ge(m2_ready, min(i + 2, GROUPS))
                wait(pe, ctx_ready, TB * i)
                for qt in range(TB):
                    last = nc.tensor.transpose(PS[:, 7, qt * P:(qt + 1) * P], OT[i % 2][:, qt * P:(qt + 1) * P], ident[:, :])
                last.then_inc(ot_t, 1)

            def ctx_transpose(b):
                for c in range(DC):
                    pe.wait_ge(ctx_ready, TB * NG * (b + 1))
                    if b == 0:
                        pe.wait_ge(max_ready, G * TB * GROUPS)
                    else:
                        pe.wait_ge(exp_done, G * TB * GROUPS)
                        pe.wait_ge(ctt_ready, 2 * b)
                    for t in range(TB):
                        last = nc.tensor.transpose(PS[:, ctt_bank(b, c), t * P:(t + 1) * P], CH[:, b * TB + t, c * P:(c + 1) * P], ident[:, :])
                    last.then_inc(ct_t, 1)

            def out_projection(b):
                pe.wait_ge(w_in["o"], 16)
                pe.wait_ge(ctt_ready, 2 * (b + 1))
                for t in range(TB):
                    if b:
                        pe.wait_ge(ao_ready, 2 * (b - 1) + t // 2 + 1)
                    for c in range(DC):
                        last = mm(PS[:, wo_bank(b, t // 2), (t % 2) * D:(t % 2 + 1) * D], ctt(b, c)[:, t * P:(t + 1) * P],
                                  W["o"][:, c, :], start=(c == 0), stop=(c == DC - 1))
                    if t % 2:
                        last.then_inc(wo_done, 1)

            for n in early:
                scores_for_max(n)
            max_transpose(0)
            for n in range(EARLY, 6 * TB):
                scores_for_max(n)
            pe.wait_ge(q1_ready, 4 * B)
            for i in range(GROUPS):
                b, g = divmod(i, NG)
                pe.wait_ge(m_in[i % 2], 32 * (i // 2 + 1))
                if i < NG:
                    pe.wait_ge(kones, g + 1)

                def scores(kt, j):
                    n = G * (TB * i + kt) + j
                    if n >= G:
                        pe.wait_ge(exp_done, n - G + 1)
                    mm(PS[:, j, :], KST[g][0:KM, j, kt * P:(kt + 1) * P], QS[g][0:KM, j, :],
                       start=True, stop=True).then_inc(st_done, 1)

                for kt in range(TB):
                    s = smax_schedule(i, kt)
                    mx = [lambda n=TB * s + qt: scores_for_max(n) for qt in range(TB)] if s is not None else \
                        [lambda: None] * TB
                    scores(kt, 0)
                    scores(kt, 1)
                    mx[0]()
                    scores(kt, 2)
                    mx[1]()
                    if kt:
                        values(i, kt - 1)
                    elif i:
                        values(i - 1, TB - 1)
                    if kt == 1 and i:
                        out_transpose(i - 1)
                    mx[2]()
                    if kt == 2 and i + 1 < GROUPS:
                        max_transpose(i + 1)
                    scores(kt, 3)
                    mx[3]()
                    if i == GROUPS - 1 and kt == 1:
                        ctx_transpose(0)
                    if i == GROUPS - 1 and kt == 3:
                        out_projection(0)
            values(GROUPS - 1, TB - 1)
            out_transpose(GROUPS - 1)

            def h2_transpose(b):
                for c in range(DC):
                    pe.wait_ge(h2_ready, TB * (b + 1))
                    pe.wait_ge(ao_ready, 2)
                    if b:
                        pe.wait_ge(h2t_ready, 2 * b)
                    for t in range(TB):
                        last = nc.tensor.transpose(PS[:, 4 + c, t * P:(t + 1) * P], CH[:, b * TB + t, c * P:(c + 1) * P], ident[:, :])
                    last.then_inc(h2_t, 1)

            def router(b):
                pe.wait_ge(w_in["router"], 16)
                pe.wait_ge(h2t_ready, 2 * (b + 1))
                if b:
                    pe.wait_ge(lg_ready, b)
                for t in range(TB):
                    for c in range(DC):
                        last = mm(PS[:, 6, t * E:(t + 1) * E], H2T[:, c, b * S + t * P:b * S + (t + 1) * P], wr[:, c, :],
                                  start=(c == 0), stop=(c == DC - 1))
                last.then_inc(lg_done, 1)

            def gate_up(b, c):
                n = IC * b + c
                if n == 0:
                    pe.wait_ge(w_in["shared"], 48)
                    pe.wait_ge(ctt_ready, 2 * B)
                    pe.wait_ge(ao_ready, 2 * B)
                if n >= 2:
                    pe.wait_ge(hs_ready, n - 1)
                for k, w in enumerate((wgate, wup)):
                    for d in range(DC):
                        last = mm(PS[:, 2 * (n % 2) + k, :], w[:, d, c * P:(c + 1) * P], H2T[:, d, b * S:(b + 1) * S],
                                  start=(d == 0), stop=(d == DC - 1))
                last.then_inc(gu_done, 1)

            def down(b):
                pe.wait_ge(hs_ready, IC * (b + 1))
                pe.wait_ge(lg_ready, B)
                for t in range(TB):
                    if b:
                        pe.wait_ge(base_ready, 2 * (b - 1) + t // 2 + 1)
                    for c in range(IC):
                        last = mm(PS[:, 6 + t // 2, (t % 2) * D:(t % 2 + 1) * D], HS[:, b % 2, c, t * P:(t + 1) * P],
                                  wdown[:, c, :], start=(c == 0), stop=(c == IC - 1))
                    if t % 2:
                        last.then_inc(down_done, 1)

            for b in range(B):
                if b:
                    out_projection(b)
                    h2_transpose(b - 1)
                if b + 1 < B:
                    ctx_transpose(b + 1)
                if b == B - 1:
                    gate_up(0, 0)
                if b:
                    router(b - 1)
            for c in range(1, AHEAD):
                gate_up(0, c)
            h2_transpose(B - 1)
            gate_up(0, AHEAD)
            router(B - 1)
            for c in range(AHEAD + 1, IC):
                gate_up(0, c)
            pe.wait_ge(dve_route, ROUTE_OH)
            pe.wait_ge(consts, 7)
            choice = OH[:, 2, :, :].rearrange("p t e -> p (t e)")
            mm(PS[:, 4, 0:NT * E], before[:, :], choice, start=True, stop=True).then_inc(route_pe, 1)
            mm(PS[:, 5, 0:NT * E], ones[:, :], choice, start=True, stop=True).then_inc(route_pe, 1)
            for b in range(1, BE):
                gate_up(b, 0)
                down(b - 1)
                for c in range(1, IC):
                    gate_up(b, c)

            pe.wait_ge(w_in["fc1"], 16 * DC * E // 2)
            pe.wait_ge(w_in["fc2"], 16 * (IE // P) * E // 2)
            pe.wait_ge(dve_route, ROUTE_EID)
            expert1 = [pe.alloc_register(f"expert1_{u}") for u in range(UN)]
            expert2 = [pe.alloc_register(f"expert2_{u}") for u in range(UN)]

            def expert_of(register):
                return bass.ds(pe.snap(register, min_val=0, max_val=E - 1), 1)

            def transpose_rows(it, u):
                pe.wait_ge(xg_in[u], (it + 1) * 16)
                wait(pe, xgt_ready, it * UN + u)
                for c in range(DC):
                    last = nc.tensor.transpose(PS[:, 0, c * P:(c + 1) * P], XG[:, u, c * P:(c + 1) * P], ident[:, :])
                last.then_inc(xg_t, 1)

            def transpose_hidden(j, u):
                pe.wait_ge(he_ready, j + 1)
                wait(pe, het_ready, j)
                for c in range(IE // P):
                    last = nc.tensor.transpose(PS[:, 4, c * P:(c + 1) * P], HE[:, u, c * P:(c + 1) * P], ident[:, :])
                last.then_inc(he_t, 1)

            def second_product(j, u):
                e = expert_of(expert2[u])
                pe.wait_ge(het_ready, j + 1)
                wait(pe, y_ready, j - UN + 1)
                for c in range(IE // P):
                    last = mm(PS[:, 5 + u, 0:D], HET[:, u, c * P:(c + 1) * P], fc2[:, c, e, :],
                              start=(c == 0), stop=(c == IE // P - 1))
                last.then_inc(y_done, 1)

            def slot_matmuls(it, u, first, last):
                j = it * UN + u
                e = expert_of(expert1[u])
                pe.wait_ge(xgt_ready, j + 1)
                wait(pe, he_ready, j - UN + 1)
                for c in range(DC):
                    last_mm = mm(PS[:, 1 + u, :], XGT[:, u, c * P:(c + 1) * P], fc1[:, c, e, :],
                                 start=(c == 0), stop=(c == DC - 1))
                last_mm.then_inc(h1_done, 1)
                if not (last and u == UN - 1):
                    pe.reg_load(expert1[(u + 1) % UN], eid[0:1, bass.ds(j + 1, 1)])
                if not (first and u == 0):
                    pe.reg_load(expert2[(u - 1) % UN], eid[0:1, bass.ds(j - 1, 1)])
                if u < UN - 1:
                    transpose_rows(it, u + 1)
                elif not last:
                    transpose_rows(it + 1, 0)
                if not (first and u == 0):
                    transpose_hidden(j - 1, (u - 1) % UN)
                if first and u == UN - 1:
                    pe.wait_ge(base_ready, 2 * BE)
                if not (first and u < 2):
                    second_product(j - 2, (u - 2) % UN)

            pe.reg_load(expert1[0], eid[0:1, 0:1])
            down(BE - 1)
            transpose_rows(0, 0)
            over_slots(pe, slot_matmuls)
            transpose_hidden(SLOTS - 1, UN - 1)
            second_product(SLOTS - 2, (SLOTS - 2) % UN)
            pe.reg_load(expert2[UN - 1], eid[0:1, SLOTS - 1:SLOTS])
            second_product(SLOTS - 1, UN - 1)
            pe.wait_ge(xgt_ready, SLOTS)
            pe.wait_ge(he_ready, SLOTS)
            for b in range(BE, B):
                for c in range(IC):
                    gate_up(b, c)
                pe.wait_ge(y_ready, SLOTS)
                down(b)


_INS = ['x', 'ctx_1024T', 'g_xattn', 'g_ffn', 'WqT', 'bq', 'WkT', 'bk', 'WvT', 'bv', 'WoT', 'bo',
        'w_router', 'fc1_w', 'fc2_w', 'gate_w', 'up_w', 'down_w']


def kernel(**inputs):
    import numpy as _np
    import concourse.bacc as _bacc
    from concourse.bass_utils import run_bass_kernel_spmd as _run

    a = {k: _np.asarray(v) for k, v in inputs.items()}
    B, S, D = a['x'].shape
    laid = [
        a['x'],
        a['ctx_1024'].reshape(B * S, D).T,
        a['g_xattn'], a['g_ffn'],
    ]
    for n in 'qkvo':
        b = a[f'L0_xattn_b{n}']
        laid += [a[f'L0_xattn_W{n}'].T, b.reshape(-1, P).T if n in 'qk' else b]
    laid += [a[f'L0_ffn_{n}'] for n in ('w_router', 'fc1_w', 'fc2_w', 'gate_w', 'up_w', 'down_w')]

    nc = _bacc.Bacc("TRN2", target_bir_lowering=False, num_devices=1)
    arrays, args = {}, []
    for name, v in zip(_INS, laid):
        v = _np.ascontiguousarray(v)
        arrays[f"in_{name}_dram"] = v
        args.append(nc.dram_tensor(f"in_{name}_dram", v.shape, mybir.dt.from_np(v.dtype), kind="ExternalInput").ap())
    args.append(nc.dram_tensor("out_dram", (B, S, D), F32, kind="ExternalOutput").ap())
    flamingo_layer(nc, *args)
    r = _run(nc, [arrays], core_ids=[0])
    return r.results[0]["out_dram"]
```
